# Optimizing a Trainium2 kernel written in Bass

```python
import numpy as np
import jax
import jax.numpy as jnp

def _softmax(x, axis=-1):
    return jax.nn.softmax(x, axis=axis)

def _gelu(x):
    return jax.nn.gelu(x, approximate=True)

def _silu(x):
    return jax.nn.silu(x)

def _sigmoid(x):
    return jax.nn.sigmoid(x)

def _layernorm(x, axis=-1, eps=1e-05):
    m = jnp.mean(x, axis=axis, keepdims=True)
    v = jnp.var(x, axis=axis, keepdims=True)
    return (x - m) / jnp.sqrt(v + eps)

def _scatter_add(tgt, idx, src, axis=0):
    return tgt.at[idx].add(src)

def _segment_sum(src, seg, n):
    return jax.ops.segment_sum(src, seg, n)
kernel_name = 'mk_gnn_resnorm_d2_gnn_r8_c98f08'

def setup_inputs(seed: int=0):
    np.random.seed(seed)
    _w = jnp.asarray

    def _rec_inputs():
        import jax
        import jax.numpy as jnp
        _gk = jax.random.key(seed)
        x = -0.0003713 + 1 * jax.random.normal(jax.random.fold_in(_gk, 1), (6250, 128), jnp.float32)
        _s = jax.random.randint(jax.random.fold_in(_gk, 2), (100000,), 0, 6250, jnp.int32)
        _d = jax.random.randint(jax.random.fold_in(_gk, 3), (100000,), 0, 6250, jnp.int32)
        _loop = jnp.arange(6250, dtype=jnp.int32)
        src = jnp.concatenate([_s, _d, _loop])
        dst = jnp.concatenate([_d, _s, _loop])
        _o = jnp.argsort(dst, stable=True)
        src = src[_o]
        dst = dst[_o]
        edge_attr_32 = 0.000135552 + 1.00015 * jax.random.normal(jax.random.fold_in(_gk, 12), (206250, 32), jnp.float32)
        edge_attr_32_n2 = 0.000135552 + 1.00015 * jax.random.normal(jax.random.fold_in(_gk, 13), (206250, 32), jnp.float32)
        return (x, src, dst, edge_attr_32, edge_attr_32_n2)
    x, src, dst, edge_attr_32, edge_attr_32_n2 = _rec_inputs()

    def _L0_gnn_setup():
        import jax, jax.numpy as jnp
        import numpy as np
        N_NODES = 12500
        N_EDGES = 200000
        D = 128
        NEG_SLOPE = 0.2
        key = jax.random.key(seed)
        k1, k2, k3, k4, k5, k6 = jax.random.split(key, 6)
        x = jax.random.normal(k1, (N_NODES, D), dtype=jnp.float32)
        src = jax.random.randint(k2, (N_EDGES,), 0, N_NODES)
        dst = jax.random.randint(k3, (N_EDGES,), 0, N_NODES)
        W = jax.random.uniform(k4, (D, D), dtype=jnp.float32, minval=-1.0, maxval=1.0) / np.sqrt(D)
        a_left = jax.random.uniform(k5, (1, D), dtype=jnp.float32, minval=-1.0, maxval=1.0) / np.sqrt(D)
        a_right = jax.random.uniform(k6, (1, D), dtype=jnp.float32, minval=-1.0, maxval=1.0) / np.sqrt(D)
        return {'x': x, 'src': src, 'dst': dst, 'W': W, 'a_left': a_left, 'a_right': a_right}
    _L0_gnn_all = _L0_gnn_setup()
    _L0_gnn_in = {k: v for k, v in _L0_gnn_all.items() if k in ('W', 'a_left', 'a_right')}
    del _L0_gnn_all

    def _L1_gnn_setup():
        import jax, jax.numpy as jnp
        import numpy as np
        N_NODES = 12500
        N_EDGES = 200000
        NODE_DIM = 128
        EDGE_DIM = 32
        OUT_DIM = 128
        key = jax.random.key(seed)
        ks = jax.random.split(key, 8)
        x = jax.random.normal(ks[0], (N_NODES, NODE_DIM), dtype=jnp.float32)
        edge_index = jax.random.randint(ks[1], (2, N_EDGES), 0, N_NODES, dtype=jnp.int64)
        edge_attr = jax.random.normal(ks[2], (N_EDGES, EDGE_DIM), dtype=jnp.float32)
        edge_t = jax.random.normal(ks[3], (N_EDGES, EDGE_DIM), dtype=jnp.float32)
        in_m = NODE_DIM + 2 * EDGE_DIM
        Wm = jax.random.uniform(ks[4], (in_m, OUT_DIM), minval=-1.0, maxval=1.0) / np.sqrt(in_m)
        bm = jax.random.uniform(ks[5], (OUT_DIM,), minval=-1.0, maxval=1.0) / np.sqrt(in_m)
        Wr = jax.random.uniform(ks[6], (NODE_DIM, OUT_DIM), minval=-1.0, maxval=1.0) / np.sqrt(NODE_DIM)
        br = jax.random.uniform(ks[7], (OUT_DIM,), minval=-1.0, maxval=1.0) / np.sqrt(NODE_DIM)
        return {'x': x, 'edge_index': edge_index, 'edge_attr': edge_attr, 'edge_t': edge_t, 'Wm': Wm, 'bm': bm, 'Wr': Wr, 'br': br}
    _L1_gnn_all = _L1_gnn_setup()
    _L1_gnn_in = {k: v for k, v in _L1_gnn_all.items() if k in ('Wm', 'bm', 'Wr', 'br')}
    del _L1_gnn_all
    return {'x': x, 'src': src, 'dst': dst, 'edge_attr_32': edge_attr_32, 'edge_attr_32_n2': edge_attr_32_n2, 'L0_gnn_W': _L0_gnn_in['W'], 'L0_gnn_a_left': _L0_gnn_in['a_left'], 'L0_gnn_a_right': _L0_gnn_in['a_right'], 'L1_gnn_Wm': _L1_gnn_in['Wm'], 'L1_gnn_bm': _L1_gnn_in['bm'], 'L1_gnn_Wr': _L1_gnn_in['Wr'], 'L1_gnn_br': _L1_gnn_in['br']}

def reference(x, src, dst, edge_attr_32, edge_attr_32_n2, L0_gnn_W, L0_gnn_a_left, L0_gnn_a_right, L1_gnn_Wm, L1_gnn_bm, L1_gnn_Wr, L1_gnn_br):
    import jax
    import jax.numpy as jnp

    def _L0_gnn_ref(x, src, dst, W, a_left, a_right):
        import jax, jax.numpy as jnp
        import numpy as np
        N_NODES = 12500
        N_EDGES = 200000
        D = 128
        NEG_SLOPE = 0.2
        n = x.shape[0]
        h = x @ W.T
        e_l = h @ a_left.T
        e_r = h @ a_right.T
        e = e_l[src] + e_r[dst]
        e = jnp.where(e >= 0, e, NEG_SLOPE * e)
        e = e[:, 0]
        m = jax.ops.segment_max(e, dst, num_segments=n)
        m = jnp.where(jnp.isfinite(m), m, 0.0)
        ex = jnp.exp(e - m[dst])
        denom = jax.ops.segment_sum(ex, dst, num_segments=n)
        alpha = ex / jnp.maximum(denom[dst], 1e-38)
        msg = h[src] * alpha[:, None]
        out = jax.ops.segment_sum(msg, dst, num_segments=n)
        return out

    def _L1_gnn_ref(x, edge_index, edge_attr, edge_t, Wm, bm, Wr, br):
        import jax, jax.numpy as jnp
        import numpy as np
        N_NODES = 12500
        N_EDGES = 200000
        NODE_DIM = 128
        EDGE_DIM = 32
        OUT_DIM = 128
        row, col = (edge_index[0], edge_index[1])
        msg = jnp.concatenate([x[col], edge_attr, edge_t], axis=1)
        agg = jax.ops.segment_sum(msg, row, num_segments=x.shape[0])
        out = agg @ Wm + bm
        out = 0.5 * out + (x @ Wr + br)
        return out
    edge_index = jnp.stack([src, dst])
    x = _layernorm(x + _L0_gnn_ref(x, src, dst, L0_gnn_W, L0_gnn_a_left, L0_gnn_a_right), axis=-1)
    x = _layernorm(x + _L1_gnn_ref(x, edge_index, edge_attr_32, edge_attr_32_n2, L1_gnn_Wm, L1_gnn_bm, L1_gnn_Wr, L1_gnn_br), axis=-1)
    return x

_drawn_inputs = setup_inputs


def setup_inputs(seed=0):
    import zlib

    import numpy as np

    out = dict(_drawn_inputs(seed))
    spreads = {}
    factors = {'L0_gnn_a_right': 5.495, 'L1_gnn_bm': 4.885}
    for name, (base, spread) in spreads.items():
        noise = np.random.default_rng([zlib.crc32(name.encode()), seed]).standard_normal(out[name].shape)
        drawn = base * np.exp(spread * noise) if base else spread * noise
        out[name] = jnp.asarray(drawn.astype(out[name].dtype))
    for name, factor in factors.items():
        out[name] = (out[name] * factor).astype(out[name].dtype)
    return out
```

```python
import concourse.bass as bass
from concourse import mybir
from contextlib import ExitStack

N = 6250
D = 128
E = 206250
FE = 64
P = 128
NB = (N + P - 1) // P
NBP = NB + 1
NP = NBP * P
PAD_NODE = NB * P
CH = 4
IT = CH * P
IT_BITS = IT.bit_length() - 1
EC = -(-(E + IT) // (P * 16)) * 16
EP = EC * P
SLOTS = 4
K = -(-(E // IT + NB - 2) // SLOTS) * SLOTS + 2
KC = K + 8
TW = D + 2
RW = D + FE + 1
LAST = N - (NB - 1) * P
HG = 3
SKIP = float(1 << 22)
SLOPE = 0.2
EPS = 1e-5
LEAST = -1e30
DST, SRC = 0, 1
assert K >= E // IT + NB and EP - IT >= E and K % SLOTS == 2 and KC <= 512 and IT == 1 << IT_BITS

f32, bf16, i32 = mybir.dt.float32, mybir.dt.bfloat16, mybir.dt.int32
ALU, ACT, AX = mybir.AluOpType, mybir.ActivationFunctionType, mybir.AxisListType


class Shared:
    pass


def at_least(eng, s, n):
    if not isinstance(n, int) or n > 0:
        eng.wait_ge(s, n)


def after(k0, c, each):
    return k0 * (each // SLOTS) + each * (c // SLOTS + 1)


def skewed(eng, step):
    step(0, 0)
    step(0, 1)
    with eng.Fori(0, K - 2, SLOTS) as k0:
        for c in range(2, 2 + SLOTS):
            step(k0, c)
    step(K - 2, 2)
    step(K - 2, 3)


def ahead(eng, load):
    for c in range(SLOTS):
        load(0, c)
    with eng.Fori(0, K - 2 - SLOTS, SLOTS) as k0:
        for c in range(SLOTS, 2 * SLOTS):
            load(k0, c)
    load(K - 2 - SLOTS, SLOTS)
    load(K - 2 - SLOTS, SLOTS + 1)


def item(k0, c):
    return not isinstance(k0, int) or 0 <= k0 + c < K


def setup_stage(nc, g, xn, xt, w, wt, a2, wm, wr, bm, br, src_h, dst_h):
    with ExitStack() as ctx:
        def sb(name, shape, dt=f32):
            return ctx.enter_context(nc.sbuf_tensor(name, shape, dt))

        def sem(name):
            return ctx.enter_context(nc.semaphore(name))

        xts = sb("xt_sb", [P, NBP, P])
        w_sb = sb("w0_sb", [P, D])
        a_sb = sb("a_sb", [P, 2])
        wx = sb("wx", [P, TW])
        ids = sb("ids", [P, EC], i32)
        hii = sb("hii", [P, EC], i32)
        hi = sb("hi", [P, 2, EC], bf16)
        here = sb("here", [P, 2, EC], bf16)
        onesb = sb("onesb", [P, EC], bf16)
        scan = sb("scan", [P, EC])
        pos = sb("pos", [P, EC])
        posi = sb("posi", [P, EC], i32)
        tri = sb("tri", [P, P])
        c128 = sb("c128", [P, P])
        cnt = sb("cnt", [P, 2, NBP])
        tot = sb("tot", [P, 2, NBP])
        run = sb("run", [P, 2, NBP])
        before = sb("before", [P, NBP])
        off = sb("off", [P, NBP])
        toti = sb("toti", [P, 2, NBP], i32)
        nit = sb("nit", [P, 2, NBP])
        itend = sb("itend", [P, 2, NBP])
        dlt = sb("dlt", [P, 2, NBP])
        junk = sb("junk", [P, NBP])
        col = sb("col", [P, 4])
        past = sb("past", [P, 2, KC])
        e0f = sb("e0f", [1, 2, KC])
        low = sb("low", [P, 3])
        padrec = sb("padrec", [P, CH, RW])
        ps = [ctx.enter_context(nc.psum_tensor(f"ps_s{i}", [P, 512], f32)) for i in range(8)]

        s_ld, s_edge, s_shift, s_tab, s_pad, s_pos = (sem(f"su_{n}") for n in ("load", "edges", "shifted", "table_stored", "pad_stored", "pos_stored"))
        s_const, s_id, s_wx, s_wxc, s_h, s_hc, s_fix = (sem(f"su_{n}") for n in ("const", "ident", "wx", "wx_copied", "h", "h_copied", "table_made"))
        s_low, s_lowt, s_lowm, s_lowb = (sem(f"su_{n}") for n in ("low", "low_turned", "low_least", "low_spread"))
        s_cnt, s_tot, s_col, s_it, s_itc, s_chain, s_posv, s_padv, s_pass = (
            sem(f"su_{n}") for n in ("counted", "totals", "columns", "items", "items_copied", "chain", "pos", "pad_made", "pass"))
        block = ctx.enter_context(nc.Block())
        groups = -(-NBP // HG)

        @block.sync
        def _(sp):
            sp.dma_start(ids[:, :], dst_h.rearrange("(p c) -> p c", p=P)).then_inc(s_edge, 16)
            for to, of in ((w_sb[:, :], w), (wx[:, 0:D], wt), (a_sb[:, :], a2),
                           (xts[:, :, :], xt.rearrange("p (b n) -> p b n", n=P)),
                           (g.x[:, :, :], xn.rearrange("(b p) d -> p b d", p=P)),
                           (g.wm1[:, :], wm[0:D, :]), (g.wm2[:, :], wm[D:D + FE, :]), (g.wr[:, :], wr),
                           (g.brow[:, 0, :], bm), (g.brow[:, 1, :], br)):
                sp.dma_start(to, of).then_inc(s_ld, 16)
            sp.wait_ge(s_shift, 1)
            sp.dma_start(ids[:, :], src_h.rearrange("(p c) -> p c", p=P)).then_inc(s_edge, 16)
            sp.wait_ge(s_fix, 2)
            sp.dma_start(g.table_d.rearrange("(b p) w -> p b w", p=P), g.table[:, :, :]).then_inc(s_tab, 16)
            sp.wait_ge(s_padv, 2)
            sp.dma_start(g.rec_d[E:E + IT, :].rearrange("(p j) w -> p j w", p=P), padrec[:, :, :]).then_inc(s_pad, 16)
            sp.wait_ge(s_posv, 1)
            sp.dma_start(g.pos_d.rearrange("(p c) -> p c", p=P), posi[:, :]).then_inc(s_pos, 16)
            sp.wait_ge(s_tab, 16)
            sp.wait_ge(s_pad, 16)
            sp.wait_ge(s_pos, 16)
            sp.wait_ge(s_ld, 160)

        @block.gpsimd
        def _(pool):
            pool.iota(g.iota[:, :], pattern=[[1, 512]], base=0, channel_multiplier=0, allow_small_or_imprecise_dtypes=True).then_inc(s_const, 1)
            pool.memset(g.ones[:, :], 1.0).then_inc(s_const, 1)
            pool.memset(onesb[:, :], 1.0).then_inc(s_const, 1)
            pool.memset(c128[:, :], float(P)).then_inc(s_const, 1)
            pool.memset(cnt[:, :, NB:NBP], 0.0).then_inc(s_const, 1)
            pool.memset(pos[:, :], SKIP + 1).then_inc(s_const, 1)
            pool.memset(g.ident[:, :], 0.0).then_inc(s_id, 1)
            pool.memset(tri[:, :], 0.0).then_inc(s_id, 1)
            pool.wait_ge(s_id, 2)
            pool.affine_select(out=g.ident[:, :], in_=g.ident[:, :], compare_op=ALU.not_equal, fill=1.0,
                               base=0, pattern=[[-1, P]], channel_multiplier=1).then_inc(s_id, 1)
            pool.affine_select(out=tri[:, :], in_=tri[:, :], compare_op=ALU.is_ge, fill=1.0,
                               base=0, pattern=[[-1, P]], channel_multiplier=1).then_inc(s_id, 1)
            pool.memset(padrec[:, :, 0:RW - 1], 0.0).then_inc(s_padv, 1)
            pool.memset(padrec[:, :, RW - 1:RW], float(PAD_NODE)).then_inc(s_padv, 1)
            pool.memset(g.acc[:, :, :], 0.0).then_inc(s_const, 1)
            pool.memset(g.erm[:, :, 1:2], LEAST).then_inc(s_const, 1)

        @block.scalar
        def _(act):
            act.wait_ge(s_wx, 1)
            nc.scalar.activation(wx[:, D:TW], ps[7][:, 0:2], ACT.Copy).then_inc(s_wxc, 1)
            for i in range(groups):
                nb = min(HG, NBP - HG * i)
                act.wait_ge(s_h, i + 1)
                nc.scalar.activation(g.table[:, HG * i:HG * i + nb, :],
                                     ps[i % 4][:, 0:nb * TW].rearrange("p (b w) -> p b w", w=TW), ACT.Copy).then_inc(s_hc, 1)

        @block.tensor
        def _(pe):
            pe.wait_ge(s_ld, 160)
            nc.tensor.matmul(ps[7][:, 0:2], w_sb[:, :], a_sb[:, :], start=True, stop=True).then_inc(s_wx, 1)
            pe.wait_ge(s_wxc, 1)
            for i in range(groups):
                at_least(pe, s_hc, i - 3)
                for n in range(min(HG, NBP - HG * i)):
                    h = nc.tensor.matmul(ps[i % 4][:, n * TW:(n + 1) * TW], xts[:, HG * i + n, :], wx[:, :], start=True, stop=True)
                h.then_inc(s_h, 1)
            pe.wait_ge(s_low, 1)
            pe.wait_ge(s_id, 4)
            pe.wait_ge(s_const, 2)
            nc.tensor.matmul(ps[6][0:1, 0:P], low[:, 0:1], g.ident[:, :], start=True, stop=True).then_inc(s_lowt, 1)
            pe.wait_ge(s_lowm, 1)
            nc.tensor.matmul(ps[6][:, P:P + 1], g.ones[0:1, :], low[0:1, 1:2], start=True, stop=True).then_inc(s_lowb, 1)
            pe.wait_ge(s_chain, 2 + 2 * NB)
            nc.tensor.matmul(ps[4][:, 0:2 * NBP], g.ones[:, :], cnt[:, :, :].rearrange("p a b -> p (a b)"), start=True, stop=True)
            nc.tensor.matmul(ps[5][:, 0:NBP], tri[:, :], cnt[:, SRC, :], start=True, stop=True).then_inc(s_tot, 1)
            for a in range(2):
                pe.wait_ge(s_col, 1)
                at_least(pe, s_itc, a)
                nc.tensor.matmul(ps[0][:, 0:KC], c128[0:NB, :], past[0:NB, a, :], start=True, stop=True)
                nc.tensor.matmul(ps[1][0:1, 0:KC], col[0:NB, 2 * a + 1:2 * a + 2], past[0:NB, a, :], start=True, stop=True).then_inc(s_it, 1)

        @block.vector
        def _(dve):
            chain = [0]

            def link(ins):
                chain[0] += 1
                ins.then_inc(s_chain, 1)
                dve.wait_ge(s_chain, chain[0])

            for a in range(2):
                dve.wait_ge(s_edge, 16 * a + 16)
                nc.vector.tensor_scalar(hii[:, :], ids[:, :], 7, None, ALU.arith_shift_right).then_inc(s_shift, 1)
                dve.wait_ge(s_shift, a + 1)
                link(nc.vector.tensor_copy(hi[:, a, :], hii[:, :]))
            dve.wait_ge(s_const, 8)
            with dve.Fori(0, NB) as b:
                for a in range(2):
                    dve.wait_ge(s_chain, b * 2 + chain[0] + a - 1)
                    nc.vector.tensor_scalar(here[:, a, :], hi[:, a, :], g.iota[:, bass.ds(b, 1)], 0.0, ALU.is_equal, ALU.add,
                                            accum_out=cnt[:, a, bass.ds(b, 1)]).then_inc(s_chain, 1)
            chain[0] += 2 * NB
            dve.wait_ge(s_hc, groups)
            link(nc.vector.tensor_copy(g.erm[:, :, 0:1], g.table[:, :, D + 1:TW]))
            nc.vector.memset(g.table[:, :, D + 1:TW], 1.0).then_inc(s_fix, 2)
            link(nc.vector.tensor_reduce(low[:, 0:1], g.table[:, :, D:D + 1].rearrange("p b w -> p (b w)"), axis=AX.X, op=ALU.min))
            nc.vector.tensor_copy(low[:, 2:3], low[:, 0:1]).then_inc(s_low, 1)
            dve.wait_ge(s_lowt, 1)
            link(nc.vector.tensor_reduce(low[0:1, 1:2], ps[6][0:1, 0:P], axis=AX.X, op=ALU.min))
            nc.vector.tensor_copy(low[0:1, 2:3], low[0:1, 1:2]).then_inc(s_lowm, 1)
            dve.wait_ge(s_lowb, 1)
            link(nc.vector.tensor_copy(g.elmin[:, :], ps[6][:, P:P + 1]))
            link(nc.vector.tensor_scalar(g.ermin[:, :, :], g.erm[:, :, 0:1], g.elmin[:, 0:1], None, ALU.add))
            dve.wait_ge(s_tot, 1)
            link(nc.vector.tensor_copy(tot[:, :, :].rearrange("p a b -> p (a b)"), ps[4][:, 0:2 * NBP]))
            link(nc.vector.tensor_scalar(toti[:, :, :], tot[:, :, :], float(IT - 1), None, ALU.add))
            link(nc.vector.tensor_scalar(toti[:, :, :], toti[:, :, :], IT_BITS, None, ALU.arith_shift_right))
            link(nc.vector.tensor_copy(nit[:, :, :], toti[:, :, :]))
            for a in range(2):
                link(nc.vector.tensor_tensor_scan(itend[:, a, :], g.ones[:, 0:NBP], nit[:, a, :], 0.0, ALU.mult, ALU.add))
            link(nc.vector.tensor_tensor_scan(run[:, SRC, :], g.ones[:, 0:NBP], tot[:, SRC, :], 0.0, ALU.mult, ALU.add))
            link(nc.vector.tensor_tensor(before[:, :], run[:, SRC, :], tot[:, SRC, :], ALU.subtract))
            link(nc.vector.tensor_tensor(off[:, :], before[:, :], ps[5][:, 0:NBP], ALU.add))
            link(nc.vector.scalar_tensor_tensor(dlt[:, :, :], nit[:, :, :], -float(IT), tot[:, :, :], ALU.mult, ALU.add))
            for a in range(2):
                for i, t in enumerate((itend, dlt)):
                    link(nc.vector.scalar_tensor_tensor(junk[:, :], t[:, a, :], 1.0, g.ident[:, 0:NBP], ALU.mult, ALU.mult,
                                                        accum_out=col[:, 2 * a + i:2 * a + i + 1]))
                link(nc.vector.tensor_scalar(past[:, a, :], g.iota[:, 0:KC], col[:, 2 * a:2 * a + 1], None, ALU.is_ge))
            nc.vector.tensor_copy(low[:, 2:3], col[:, 0:1]).then_inc(s_col, 1)
            for a, cap in ((DST, EP - IT), (SRC, E)):
                dve.wait_ge(s_it, a + 1)
                link(nc.vector.tensor_copy(g.b128[:, a, :], ps[0][:, 0:KC]))
                link(nc.vector.tensor_scalar(g.bt[:, a, :], g.b128[0:1, a, :], 1.0 / P, None, ALU.mult))
                link(nc.vector.scalar_tensor_tensor(e0f[:, a, :], g.iota[0:1, 0:KC], float(IT), ps[1][0:1, 0:KC], ALU.mult, ALU.add))
                nc.vector.tensor_scalar(g.e0t[:, a, :], e0f[:, a, :], float(cap), None, ALU.min).then_inc(s_itc, 1)
            with dve.Fori(0, NB) as b:
                dve.wait_ge(s_chain, b * 3 + chain[0])
                nc.vector.tensor_scalar(here[:, 0, :], hi[:, SRC, :], g.iota[:, bass.ds(b, 1)], None, ALU.is_equal).then_inc(s_chain, 1)
                dve.wait_ge(s_chain, b * 3 + chain[0] + 1)
                nc.vector.tensor_tensor_scan(scan[:, :], onesb[:, :], here[:, 0, :], off[:, bass.ds(b, 1)], ALU.mult, ALU.add).then_inc(s_chain, 1)
                dve.wait_ge(s_chain, b * 3 + chain[0] + 2)
                dve.sem_inc(s_pass, 1)
                nc.vector.copy_predicated(pos[:, :], here[:, 0, :].bitcast(mybir.dt.uint16), scan[:, :]).then_inc(s_chain, 1)
            chain[0] += 3 * NB
            dve.wait_ge(s_chain, chain[0])
            nc.vector.tensor_scalar(posi[:, :], pos[:, :], -1.0, None, ALU.add).then_inc(s_posv, 1)


def first_layer_stage(nc, g, meta_h):
    with ExitStack() as ctx:
        def sb(name, shape, dt=f32):
            return ctx.enter_context(nc.sbuf_tensor(name, shape, dt))

        def sem(name):
            return ctx.enter_context(nc.semaphore(name))

        meta = sb("meta1", [P, SLOTS, CH, 2], i32)
        rows = sb("rows", [P, SLOTS, CH, TW])
        rel = sb("rel1", [P, 2, CH])
        elp = sb("elp", [P, 2, CH])
        hot = sb("hot1", [P, 2, CH, P])
        hot_t = sb("hot_t1", [P, 2, CH * P])
        diag = sb("diag", [P, 2, CH, P])
        wgt = sb("wgt", [P, 2, CH, P])
        mx = sb("mx", [P, 2, 5])
        sc = sb("sc", [P, 2, 4, CH])
        fade = sb("fade", [P, 2, 1])
        ps_t = ctx.enter_context(nc.psum_tensor("ps_t", [P, 512], f32))
        ps_x = [ctx.enter_context(nc.psum_tensor(f"ps_x{i}", [P, 512], f32)) for i in range(2)]
        ps_o = [ctx.enter_context(nc.psum_tensor(f"ps_o{i}", [P, 512], f32)) for i in range(2)]
        ps_e = [ctx.enter_context(nc.psum_tensor(f"ps_e{i}", [P, 512], f32)) for i in range(2)]

        meta_in = [sem(f"meta_in{i}") for i in range(SLOTS)]
        gathered = [sem(f"gathered{i}") for i in range(SLOTS)]
        (s_rel, s_elp, s_hot, s_turned, s_hot_t, s_diag, s_spread, s_max, s_sum, s_leaky, s_m, s_grown, s_kept,
         s_picked, s_z, s_lz, s_q, s_p, s_wgt, s_out, s_fade, s_acc, s_pass) = (
            sem(f"l1_{n}") for n in ("rel", "elp", "hot", "turned", "hot_t", "diag", "spread", "max", "sum", "leaky", "m",
                                     "grown", "kept", "picked", "z", "lz", "q", "p", "wgt", "out", "fade", "acc", "pass"))
        block = ctx.enter_context(nc.Block())

        @block.sync
        def _(sp):
            def load(k0, c):
                s = c % SLOTS
                e0 = sp.value_load(g.e0t[0:1, DST, bass.ds(k0 + c, 1)], min_val=0, max_val=EP - IT)
                at_least(sp, s_rel, k0 + c - 3)
                at_least(sp, s_out, k0 + c - 3)
                sp.dma_start(meta[:, s, :, :], meta_h[bass.ds(e0, IT), :].rearrange("(p j) w -> p j w", p=P)).then_inc(meta_in[s], 16)

            ahead(sp, load)

        @block.gpsimd
        def _(pool):
            def gather(k0, c):
                s = c % SLOTS
                pool.wait_ge(meta_in[s], after(k0, c, 16))
                at_least(pool, s_out, k0 + c - 3)
                pool.sem_inc(s_pass, 1)
                for j in range(CH):
                    pool.indirect_dma_start(out=rows[:, s, j, :], out_offset=None, in_=g.table_d,
                                            in_offset=bass.IndirectOffsetOnAxis(ap=meta[:, s, j, 0:1], axis=0)).then_inc(gathered[s], 16)

            ahead(pool, gather)

        @block.scalar
        def _(act):
            def step(k0, c):
                k = k0 + c
                u, v = c % 2, (c + 1) % 2
                if item(k0, c - 1):
                    act.wait_ge(s_grown, k)
                    at_least(act, s_acc, k - 2)
                    nc.scalar.activation(fade[:, v, :], mx[:, v, 4:5], ACT.Exp).then_inc(s_fade, 1)
                    act.wait_ge(s_q, k)
                    at_least(act, s_wgt, k - 2)
                    nc.scalar.activation(sc[:, v, 3, :], sc[:, v, 2, :], ACT.Exp).then_inc(s_p, 1)
                if item(k0, c):
                    act.wait_ge(s_elp, k + 1)
                    at_least(act, s_spread, k - 1)
                    for j in range(CH):
                        nc.scalar.activation(diag[:, u, j, :], g.ident[:, :], ACT.Copy, scale=elp[:, u, j:j + 1]).then_inc(s_diag, 1)
                    act.wait_ge(s_turned, k + 1)
                    at_least(act, s_picked, k - 1)
                    nc.scalar.activation(hot_t[:, u, :], ps_t[:, :], ACT.Copy).then_inc(s_hot_t, 1)

            skewed(act, step)

        @block.tensor
        def _(pe):
            def step(k0, c):
                k = k0 + c
                u, v = c % 2, (c + 1) % 2
                if item(k0, c - 1):
                    b = pe.value_load(g.bt[0:1, DST, bass.ds(k0 + c - 1, 1)], min_val=0, max_val=NB)
                    pe.wait_ge(s_kept, k)
                    pe.wait_ge(s_hot_t, k)
                    at_least(pe, s_q, k - 2)
                    for j in range(CH):
                        mm = nc.tensor.matmul(ps_e[v][:, 2 * j:2 * j + 2], hot_t[:, v, j * P:(j + 1) * P], g.erm[:, bass.ds(b, 1), :], start=True, stop=True)
                    mm.then_inc(s_picked, 1)
                if item(k0, c):
                    pe.wait_ge(s_hot, k + 1)
                    at_least(pe, s_hot_t, k)
                    for j in range(CH):
                        mm = nc.tensor.transpose(ps_t[:, j * P:(j + 1) * P], hot[:, u, j, :], g.ident[:, :])
                    mm.then_inc(s_turned, 1)
                    pe.wait_ge(s_diag, k * CH + CH)
                    at_least(pe, s_max, k - 1)
                    for j in range(CH):
                        mm = nc.tensor.matmul(ps_x[u][:, j * P:(j + 1) * P], hot[:, u, j, :], diag[:, u, j, :], start=True, stop=True)
                    mm.then_inc(s_spread, 1)
                if item(k0, c - 1):
                    pe.wait_ge(s_wgt, k)
                    at_least(pe, s_acc, k - 2)
                    for j in range(CH):
                        mm = nc.tensor.matmul(ps_o[v][:, 0:TW], wgt[:, v, j, :], rows[:, (c - 1) % SLOTS, j, :], start=j == 0, stop=j == CH - 1)
                    mm.then_inc(s_out, 1)

            skewed(pe, step)

        @block.vector
        def _(dve):
            def load_block(k0, c):
                return dve.value_load(g.bt[0:1, DST, bass.ds(k0 + c, 1)], min_val=0, max_val=NB)

            def step(k0, c):
                k = k0 + c
                u, v = c % 2, (c + 1) % 2
                s, s1 = c % SLOTS, (c - 1) % SLOTS
                b1 = load_block(k0, c - 1) if item(k0, c - 1) else None
                b2 = load_block(k0, c - 2) if item(k0, c - 2) else None
                if b1 is not None:
                    b1 = bass.ds(b1, 1)
                    dve.wait_ge(s_spread, k)
                    nc.vector.tensor_reduce(mx[:, v, 0:1], ps_x[v][:, :], axis=AX.X, op=ALU.max).then_inc(s_max, 1)
                    dve.wait_ge(s_max, k)
                    nc.vector.tensor_tensor(mx[:, v, 1:2], mx[:, v, 0:1], g.ermin[:, b1, 0], ALU.add).then_inc(s_sum, 1)
                    dve.wait_ge(s_sum, k)
                    nc.vector.scalar_tensor_tensor(mx[:, v, 2:3], mx[:, v, 1:2], SLOPE, mx[:, v, 1:2], ALU.mult, ALU.max).then_inc(s_leaky, 1)
                    dve.wait_ge(s_leaky, k)
                    at_least(dve, s_kept, k - 1)
                    nc.vector.tensor_tensor(mx[:, v, 3:4], mx[:, v, 2:3], g.erm[:, b1, 1], ALU.max).then_inc(s_m, 1)
                    dve.wait_ge(s_m, k)
                    at_least(dve, s_fade, k - 2)
                    nc.vector.tensor_tensor(mx[:, v, 4:5], g.erm[:, b1, 1], mx[:, v, 3:4], ALU.subtract).then_inc(s_grown, 1)
                    at_least(dve, s_picked, k - 1)
                    dve.wait_ge(s_grown, k)
                    nc.vector.tensor_tensor(g.erm[:, b1, 1], g.erm[:, b1, 1], mx[:, v, 3:4], ALU.max).then_inc(s_kept, 1)
                if item(k0, c):
                    dve.wait_ge(meta_in[s], after(k0, c, 16))
                    nc.vector.tensor_scalar(rel[:, u, :], meta[:, s, :, 1], g.b128[:, DST, bass.ds(k, 1)], None, ALU.subtract).then_inc(s_rel, 1)
                    dve.wait_ge(gathered[s], after(k0, c, 16 * CH))
                    at_least(dve, s_diag, k * CH - CH)
                    nc.vector.tensor_scalar(elp[:, u, :], rows[:, s, :, D], g.elmin[:, 0:1], None, ALU.subtract).then_inc(s_elp, 1)
                    dve.wait_ge(s_rel, k + 1)
                    at_least(dve, s_spread, k - 1)
                    nc.vector.tensor_tensor(hot[:, u, :, :], g.iota[:, 0:P].unsqueeze(1).to_broadcast([P, CH, P]),
                                            rel[:, u, :].unsqueeze(2).to_broadcast([P, CH, P]), ALU.is_equal).then_inc(s_hot, 1)
                if b1 is not None:
                    er_m = ps_e[v][:, 0:2 * CH].rearrange("p (j w) -> p j w", w=2)
                    dve.wait_ge(s_picked, k)
                    nc.vector.tensor_tensor(sc[:, v, 0, :], rows[:, s1, :, D], er_m[:, :, 0], ALU.add).then_inc(s_z, 1)
                    dve.wait_ge(s_z, k)
                    nc.vector.scalar_tensor_tensor(sc[:, v, 1, :], sc[:, v, 0, :], SLOPE, sc[:, v, 0, :], ALU.mult, ALU.max).then_inc(s_lz, 1)
                    dve.wait_ge(s_lz, k)
                    at_least(dve, s_p, k - 2)
                    nc.vector.tensor_tensor(sc[:, v, 2, :], sc[:, v, 1, :], er_m[:, :, 1], ALU.subtract).then_inc(s_q, 1)
                if b2 is not None:
                    b2 = bass.ds(b2, 1)
                    dve.wait_ge(s_out, k - 1)
                    dve.wait_ge(s_fade, k - 1)
                    at_least(dve, s_acc, k - 2)
                    nc.vector.scalar_tensor_tensor(g.acc[:, b2, :], g.acc[:, b2, :], fade[:, u, :],
                                                   ps_o[u][:, 0:TW].unsqueeze(1), ALU.mult, ALU.add).then_inc(s_acc, 1)
                if b1 is not None:
                    dve.wait_ge(s_p, k)
                    at_least(dve, s_out, k - 2)
                    nc.vector.scalar_tensor_tensor(wgt[:, v, :, :], sc[:, v, 3, :].unsqueeze(2).to_broadcast([P, CH, P]), 1.0,
                                                   hot[:, v, :, :], ALU.min, ALU.mult).then_inc(s_wgt, 1)

            skewed(dve, step)


def normalise(nc, dve, act, val, tmp, stat, s_v, s_a, link=None):
    pass


def norm_stage(nc, g, val, name, first):
    with ExitStack() as ctx:
        tmp = ctx.enter_context(nc.sbuf_tensor(f"{name}_tmp", [P, NB, D], f32))
        sq = ctx.enter_context(nc.sbuf_tensor(f"{name}_sq", [P, NB, D], f32)) if False else None
        st = ctx.enter_context(nc.sbuf_tensor(f"{name}_st", [P, 5, NB], f32))
        s_sq, s_root, s_v, s_var, s_sqr = (ctx.enter_context(nc.semaphore(f"{name}_{n}")) for n in ("sq", "root", "v", "var", "centred"))
        block = ctx.enter_context(nc.Block())

        @block.scalar
        def _(act):
            act.wait_ge(s_sqr, 1)
            nc.scalar.activation(tmp[:, :, :], val[:, 0:NB, :], ACT.Square).then_inc(s_sq, 1)
            act.wait_ge(s_var, 1)
            nc.scalar.activation(st[:, 3, :], st[:, 2, :], ACT.Sqrt).then_inc(s_root, 1)

        @block.vector
        def _(dve):
            chain = [0]

            def link(ins):
                chain[0] += 1
                ins.then_inc(s_v, 1)
                dve.wait_ge(s_v, chain[0])

            def spread(i):
                return st[:, i, :].unsqueeze(2).to_broadcast([P, NB, D])

            v = val[:, 0:NB, :]
            if first:
                link(nc.vector.tensor_scalar(st[:, 0, :], g.acc[:, 0:NB, TW - 1], 1e-38, None, ALU.max))
                link(nc.vector.reciprocal(st[:, 1, :], st[:, 0, :]))
                link(nc.vector.tensor_tensor(tmp[:, :, :], g.acc[:, 0:NB, 0:D], spread(1), ALU.mult))
                link(nc.vector.tensor_tensor(v, v, tmp[:, :, :], ALU.add))
            link(nc.vector.tensor_reduce(st[:, 0, :], v, axis=AX.X, op=ALU.add))
            link(nc.vector.tensor_scalar(st[:, 1, :], st[:, 0, :], 1.0 / D, None, ALU.mult))
            link(nc.vector.tensor_tensor(v, v, spread(1), ALU.subtract))
            nc.vector.tensor_copy(st[:, 4, 0:1], st[:, 1, 0:1]).then_inc(s_sqr, 1)
            if first:
                nc.vector.memset(g.acc2[:, :, :], 0.0)
            dve.wait_ge(s_sq, 1)
            link(nc.vector.tensor_reduce(st[:, 0, :], tmp[:, :, :], axis=AX.X, op=ALU.add))
            nc.vector.tensor_scalar(st[:, 2, :], st[:, 0, :], 1.0 / D, EPS, ALU.mult, ALU.add).then_inc(s_var, 1)
            dve.wait_ge(s_root, 1)
            link(nc.vector.reciprocal(st[:, 4, :], st[:, 3, :]))
            nc.vector.tensor_tensor(v, v, spread(4), ALU.mult)


def record_stage(nc, g, meta_h, feat_h):
    with ExitStack() as ctx:
        def sb(name, shape, dt=f32):
            return ctx.enter_context(nc.sbuf_tensor(name, shape, dt))

        def sem(name):
            return ctx.enter_context(nc.semaphore(name))

        meta = sb("meta2", [P, SLOTS, CH, 2], i32)
        posn = sb("posn", [P, SLOTS, CH], i32)
        rec = sb("rec2", [P, SLOTS, CH, RW])
        rel = sb("rel2", [P, 2, CH])
        far = sb("far", [P, 2, 2, CH])
        hot = sb("hot2", [P, 2, CH, P])
        hot_t = sb("hot_t2", [P, 2, CH * P])
        to = sb("to", [P, SLOTS, CH], i32)
        ps_t = [ctx.enter_context(nc.psum_tensor(f"ps_t{i}", [P, 512], f32)) for i in range(2)]
        ps_g = [ctx.enter_context(nc.psum_tensor(f"ps_g{i}", [P, 512], f32)) for i in range(2)]
        edge_in = [sem(f"edge_in{i}") for i in range(SLOTS)]
        scattered = [sem(f"scattered{i}") for i in range(SLOTS)]
        (s_rel, s_hot, s_src, s_far, s_out_of, s_to, s_turned, s_hot_t, s_got, s_rec, s_pass) = (
            sem(f"rc_{n}") for n in ("rel", "hot", "src", "far", "outside", "to", "turned", "hot_t", "got", "rec", "pass"))
        block = ctx.enter_context(nc.Block())

        @block.sync
        def _(sp):
            def load(k0, c):
                s = c % SLOTS
                e0 = sp.value_load(g.e0t[0:1, DST, bass.ds(k0 + c, 1)], min_val=0, max_val=EP - IT)
                if not isinstance(k0, int) or k0 + c >= SLOTS:
                    sp.wait_ge(scattered[s], after(k0, c - SLOTS, 16 * CH))
                sp.dma_start(meta[:, s, :, :], meta_h[bass.ds(e0, IT), :].rearrange("(p j) w -> p j w", p=P)).then_inc(edge_in[s], 16)
                sp.dma_start(posn[:, s, :], g.pos_d[bass.ds(e0, IT)].rearrange("(p j) -> p j", p=P)).then_inc(edge_in[s], 16)
                sp.dma_start(rec[:, s, :, D:D + FE], feat_h[bass.ds(e0, IT), :].rearrange("(p j) w -> p j w", p=P)).then_inc(edge_in[s], 16)

            ahead(sp, load)
            for s in range(SLOTS):
                sp.wait_ge(scattered[s], 16 * CH * len(range(s, K, SLOTS)))

        @block.gpsimd
        def _(pool):
            def scatter(k0, c):
                s = c % SLOTS
                pool.wait_ge(s_to, k0 + c + 1)
                pool.wait_ge(s_src, k0 + c + 1)
                pool.wait_ge(s_rec, k0 + c + 1)
                pool.sem_inc(s_pass, 1)
                for j in range(CH):
                    pool.indirect_dma_start(out=g.rec_d, out_offset=bass.IndirectOffsetOnAxis(ap=to[:, s, j:j + 1], axis=0),
                                            in_=rec[:, s, j, :], in_offset=None,
                                            bounds_check=E - 1, oob_is_err=False).then_inc(scattered[s], 16)

            ahead(pool, scatter)

        @block.scalar
        def _(act):
            def step(k0, c):
                k = k0 + c
                u, v, s1 = c % 2, (c + 1) % 2, (c - 1) % SLOTS
                if item(k0, c):
                    act.wait_ge(s_turned, k + 1)
                    at_least(act, s_got, k - 1)
                    nc.scalar.activation(hot_t[:, u, :], ps_t[u][:, :], ACT.Copy).then_inc(s_hot_t, 1)
                if item(k0, c - 1):
                    act.wait_ge(s_got, k)
                    act.wait_ge(edge_in[s1], after(k0, c - 1, 48))
                    nc.scalar.activation(rec[:, s1, :, 0:D], ps_g[v][:, :].rearrange("p (j n) -> p j n", n=P), ACT.Copy).then_inc(s_rec, 1)

            skewed(act, step)

        @block.tensor
        def _(pe):
            def step(k0, c):
                k = k0 + c
                u, v = c % 2, (c + 1) % 2
                b = pe.value_load(g.bt[0:1, DST, bass.ds(k0 + c - 1, 1)], min_val=0, max_val=NB) if item(k0, c - 1) else None
                if item(k0, c):
                    pe.wait_ge(s_hot, k + 1)
                    at_least(pe, s_hot_t, k - 1)
                    for j in range(CH):
                        mm = nc.tensor.transpose(ps_t[u][:, j * P:(j + 1) * P], hot[:, u, j, :], g.ident[:, :])
                    mm.then_inc(s_turned, 1)
                if b is not None:
                    pe.wait_ge(s_hot_t, k)
                    at_least(pe, s_rec, k - 2)
                    for j in range(CH):
                        mm = nc.tensor.matmul(ps_g[v][:, j * P:(j + 1) * P], hot_t[:, v, j * P:(j + 1) * P], g.x[:, bass.ds(b, 1), :], start=True, stop=True)
                    mm.then_inc(s_got, 1)

            skewed(pe, step)

        @block.vector
        def _(dve):
            def step(k0, c):
                k = k0 + c
                u, s = c % 2, c % SLOTS
                dve.wait_ge(edge_in[s], after(k0, c, 48))
                nc.vector.tensor_scalar(rel[:, u, :], meta[:, s, :, 1], g.b128[:, DST, bass.ds(k, 1)], None, ALU.subtract).then_inc(s_rel, 1)
                nc.vector.tensor_copy(rec[:, s, :, RW - 1], meta[:, s, :, 0]).then_inc(s_src, 1)
                dve.wait_ge(s_rel, k + 1)
                at_least(dve, s_turned, k - 1)
                nc.vector.tensor_tensor(hot[:, u, :, :], g.iota[:, 0:P].unsqueeze(1).to_broadcast([P, CH, P]),
                                        rel[:, u, :].unsqueeze(2).to_broadcast([P, CH, P]), ALU.is_equal).then_inc(s_hot, 1)
                nc.vector.scalar_tensor_tensor(far[:, u, 0, :], rel[:, u, :], -(P - 1.0), rel[:, u, :], ALU.add, ALU.mult).then_inc(s_far, 1)
                dve.wait_ge(s_far, k + 1)
                nc.vector.tensor_scalar(far[:, u, 1, :], far[:, u, 0, :], 0.0, SKIP, ALU.is_gt, ALU.mult).then_inc(s_out_of, 1)
                dve.wait_ge(s_out_of, k + 1)
                nc.vector.tensor_tensor(to[:, s, :], posn[:, s, :], far[:, u, 1, :], ALU.add).then_inc(s_to, 1)

            ahead(dve, step)


def sum_stage(nc, g):
    with ExitStack() as ctx:
        def sb(name, shape, dt=f32):
            return ctx.enter_context(nc.sbuf_tensor(name, shape, dt))

        def sem(name):
            return ctx.enter_context(nc.semaphore(name))

        rec = sb("rec3", [P, SLOTS, CH, RW])
        rel = sb("rel3", [P, 2, CH])
        hot = sb("hot3", [P, 2, CH, P])
        ps_a = [ctx.enter_context(nc.psum_tensor(f"ps_a{i}", [P, 512], f32)) for i in range(2)]
        rec_in = [sem(f"rec_in{i}") for i in range(SLOTS)]
        s_rel, s_hot, s_sum, s_acc = (sem(f"sm_{n}") for n in ("rel", "hot", "sum", "acc"))
        block = ctx.enter_context(nc.Block())

        @block.sync
        def _(sp):
            def load(k0, c):
                s = c % SLOTS
                e0 = sp.value_load(g.e0t[0:1, SRC, bass.ds(k0 + c, 1)], min_val=0, max_val=E)
                at_least(sp, s_sum, k0 + c - 3)
                sp.dma_start(rec[:, s, :, :], g.rec_d[bass.ds(e0, IT), :].rearrange("(p j) w -> p j w", p=P)).then_inc(rec_in[s], 16)

            ahead(sp, load)

        @block.tensor
        def _(pe):
            def step(k0, c):
                k = k0 + c
                u, s = c % 2, c % SLOTS
                pe.wait_ge(s_hot, k + 1)
                at_least(pe, s_acc, k - 1)
                for j in range(CH):
                    mm = nc.tensor.matmul(ps_a[u][:, 0:D + FE], hot[:, u, j, :], rec[:, s, j, 0:D + FE], start=j == 0, stop=j == CH - 1)
                mm.then_inc(s_sum, 1)

            ahead(pe, step)

        @block.vector
        def _(dve):
            def step(k0, c):
                k = k0 + c
                u, v, s = c % 2, (c + 1) % 2, c % SLOTS
                b = dve.value_load(g.bt[0:1, SRC, bass.ds(k0 + c - 1, 1)], min_val=0, max_val=NB) if item(k0, c - 1) else None
                if item(k0, c):
                    dve.wait_ge(rec_in[s], after(k0, c, 16))
                    nc.vector.tensor_scalar(rel[:, u, :], rec[:, s, :, RW - 1], g.b128[:, SRC, bass.ds(k, 1)], None, ALU.subtract).then_inc(s_rel, 1)
                    dve.wait_ge(s_rel, k + 1)
                    at_least(dve, s_sum, k - 1)
                    nc.vector.tensor_tensor(hot[:, u, :, :], g.iota[:, 0:P].unsqueeze(1).to_broadcast([P, CH, P]),
                                            rel[:, u, :].unsqueeze(2).to_broadcast([P, CH, P]), ALU.is_equal).then_inc(s_hot, 1)
                if b is not None:
                    b = bass.ds(b, 1)
                    dve.wait_ge(s_sum, k)
                    at_least(dve, s_acc, k - 1)
                    nc.vector.tensor_tensor(g.acc2[:, b, :], g.acc2[:, b, :], ps_a[v][:, 0:D + FE].unsqueeze(1), ALU.add).then_inc(s_acc, 1)

            skewed(dve, step)


def output_stage(nc, g):
    with ExitStack() as ctx:
        def sem(name):
            return ctx.enter_context(nc.semaphore(name))

        turned = ctx.enter_context(nc.sbuf_tensor("turned", [P, 2, 3, P], f32))
        ps_t = [ctx.enter_context(nc.psum_tensor(f"ps_f{i}", [P, 512], f32)) for i in range(2)]
        ps_y = [ctx.enter_context(nc.psum_tensor(f"ps_y{i}", [P, 512], f32)) for i in range(2)]
        s_half, s_turned, s_cp, s_y, s_res, s_bias = (sem(f"ot_{n}") for n in ("halved", "turned", "copied", "y", "added", "bias"))
        block = ctx.enter_context(nc.Block())

        @block.scalar
        def _(act):
            nc.scalar.activation(g.wm1[:, :], g.wm1[:, :], ACT.Copy, scale=0.5).then_inc(s_half, 1)
            nc.scalar.activation(g.wm2[:, :], g.wm2[:, :], ACT.Copy, scale=0.5).then_inc(s_half, 1)
            for b in range(NB):
                u = b % 2
                act.wait_ge(s_turned, b + 1)
                at_least(act, s_y, b - 1)
                nc.scalar.activation(turned[:, u, 0:2, :], ps_t[u][:, 0:2 * P].rearrange("p (i n) -> p i n", n=P), ACT.Copy).then_inc(s_cp, 1)
                nc.scalar.activation(turned[0:FE, u, 2, :], ps_t[u][0:FE, 2 * P:3 * P], ACT.Copy).then_inc(s_cp, 1)

        @block.tensor
        def _(pe):
            def turn(b):
                u = b % 2
                at_least(pe, s_cp, 2 * b - 2)
                nc.tensor.transpose(ps_t[u][:, 0:P], g.acc2[:, b, 0:D], g.ident[:, :])
                nc.tensor.transpose(ps_t[u][:, P:2 * P], g.x[:, b, :], g.ident[:, :])
                nc.tensor.transpose(ps_t[u][0:FE, 2 * P:3 * P], g.acc2[:, b, D:D + FE], g.ident[:, :]).then_inc(s_turned, 1)

            turn(0)
            pe.wait_ge(s_half, 2)
            pe.wait_ge(s_bias, 1)
            for b in range(NB):
                u = b % 2
                if b + 1 < NB:
                    turn(b + 1)
                pe.wait_ge(s_cp, 2 * b + 2)
                at_least(pe, s_res, b - 1)
                nc.tensor.matmul(ps_y[u][:, 0:D], turned[:, u, 0, :], g.wm1[:, :], start=True, stop=False)
                nc.tensor.matmul(ps_y[u][:, 0:D], turned[:, u, 1, :], g.wr[:, :], start=False, stop=False)
                nc.tensor.matmul(ps_y[u][:, 0:D], turned[0:FE, u, 2, :], g.wm2[:, :], start=False, stop=False)
                nc.tensor.matmul(ps_y[u][:, 0:D], g.ones[0:1, :], g.brow[:, 2, :], start=False, stop=True).then_inc(s_y, 1)

        @block.vector
        def _(dve):
            nc.vector.scalar_tensor_tensor(g.brow[:, 2, :], g.brow[:, 0, :], 0.5, g.brow[:, 1, :], ALU.mult, ALU.add).then_inc(s_bias, 1)
            for b in range(NB):
                dve.wait_ge(s_y, b + 1)
                nc.vector.tensor_tensor(g.y[:, b, :], g.x[:, b, :], ps_y[b % 2][:, 0:D], ALU.add).then_inc(s_res, 1)


def gnn_two_layers(nc, xn, xt, w, wt, a2, wm, wr, bm, br, src_h, dst_h, meta_h, feat_h, out):
    with ExitStack() as ctx:
        def sb(name, shape, dt=f32):
            return ctx.enter_context(nc.sbuf_tensor(name, shape, dt))

        g = Shared()
        g.table_d = nc.dram_tensor("node_table", (NP, TW), f32).ap()
        g.pos_d = nc.dram_tensor("edge_position", (EP,), i32).ap()
        g.rec_d = nc.dram_tensor("records", (E + IT, RW), f32).ap()
        g.x = sb("x", [P, NBP, D])
        g.acc = sb("acc", [P, NBP, TW])
        g.y = g.acc[:, :, 0:D]
        g.acc2 = sb("acc2", [P, NBP, D + FE])
        g.table = g.acc2[:, :, 0:TW]
        g.erm = sb("erm", [P, NBP, 2])
        g.ermin = sb("ermin", [P, NBP, 1])
        g.elmin = sb("elmin", [P, 1])
        g.ident = sb("ident", [P, P])
        g.ones = sb("ones", [P, P])
        g.iota = sb("iota", [P, 512])
        g.wm1 = sb("wm1", [P, D])
        g.wm2 = sb("wm2", [FE, D])
        g.wr = sb("wr_sb", [P, D])
        g.brow = sb("brow", [1, 3, D])
        g.b128 = sb("b128", [P, 2, KC])
        g.e0t = sb("e0t", [1, 2, KC], i32)
        g.bt = sb("bt", [1, 2, KC], i32)

        setup_stage(nc, g, xn, xt, w, wt, a2, wm, wr, bm, br, src_h, dst_h)
        first_layer_stage(nc, g, meta_h)
        norm_stage(nc, g, g.x, "n1", True)
        record_stage(nc, g, meta_h, feat_h)
        sum_stage(nc, g)
        output_stage(nc, g)
        norm_stage(nc, g, g.y, "n2", False)
        s_out = ctx.enter_context(nc.semaphore("stored"))
        block = ctx.enter_context(nc.Block())

        @block.sync
        def _(sp):
            sp.dma_start(out[0:(NB - 1) * P, :].rearrange("(b p) d -> p b d", p=P), g.y[:, 0:NB - 1, :]).then_inc(s_out, 16)
            sp.dma_start(out[(NB - 1) * P:N, :], g.y[0:LAST, NB - 1, :]).then_inc(s_out, 16)
            sp.wait_ge(s_out, 32)


def kernel(x, src, dst, edge_attr_32, edge_attr_32_n2, L0_gnn_W, L0_gnn_a_left, L0_gnn_a_right,
           L1_gnn_Wm, L1_gnn_bm, L1_gnn_Wr, L1_gnn_br):
    import numpy as np
    import concourse.bacc as bacc
    from concourse.bass_utils import run_bass_kernel_spmd

    def rows(a, n, fill):
        a = np.asarray(a)
        return np.concatenate([a, np.full((n - len(a),) + a.shape[1:], fill, a.dtype)])

    xp = rows(x, NP, 0)
    sp, dp = rows(src, EP, PAD_NODE), rows(dst, EP, PAD_NODE)
    ins = {
        "xn": xp, "xt": np.ascontiguousarray(xp.T),
        "w": np.asarray(L0_gnn_W), "wt": np.ascontiguousarray(np.asarray(L0_gnn_W).T),
        "a2": np.ascontiguousarray(np.concatenate([np.asarray(L0_gnn_a_left), np.asarray(L0_gnn_a_right)]).T),
        "wm": np.asarray(L1_gnn_Wm), "wr": np.asarray(L1_gnn_Wr),
        "bm": np.asarray(L1_gnn_bm)[None, :], "br": np.asarray(L1_gnn_br)[None, :],
        "src_h": sp, "dst_h": dp, "meta_h": np.stack([sp, dp], axis=1),
        "feat_h": rows(np.concatenate([np.asarray(edge_attr_32), np.asarray(edge_attr_32_n2)], axis=1), EP, 0),
    }
    nc = bacc.Bacc("TRN2", target_bir_lowering=False, num_devices=1)
    args = [nc.dram_tensor(n, a.shape, mybir.dt.from_np(a.dtype), kind="ExternalInput").ap() for n, a in ins.items()]
    args.append(nc.dram_tensor("out", (N, D), f32, kind="ExternalOutput").ap())
    gnn_two_layers(nc, *args)
    r = run_bass_kernel_spmd(nc, [ins], core_ids=[0])
    return r.results[0]["out"]
```

```python
import concourse.bass as bass
from concourse import mybir
from contextlib import ExitStack

N = 6250
D = 128
E = 206250
FE = 64
P = 128
NB = (N + P - 1) // P
NBP = NB + 1
NP = NBP * P
PAD_NODE = NB * P
CH = 4
IT = CH * P
IT_BITS = IT.bit_length() - 1
EC = -(-(E + IT) // (P * 16)) * 16
EP = EC * P
SLOTS = 6
DEPTH = 3
K = -(-(E // IT + NB - DEPTH) // SLOTS) * SLOTS + DEPTH
KC = K + 2 * SLOTS
TW = D + 3
SW = D + 2
RW = D + 1
PARTS = 3
LAST = N - (NB - 1) * P
HG = 3
SKIP = float(1 << 22)
SLOPE = 0.2
EPS = 1e-5
LEAST = -1e30
MOST = 1e38
DST, SRC = 0, 1
assert K >= E // IT + NB and EP - IT >= E and K % SLOTS == DEPTH and KC <= 512 and IT == 1 << IT_BITS

f32, bf16, i32 = mybir.dt.float32, mybir.dt.bfloat16, mybir.dt.int32
ALU, ACT, AX = mybir.AluOpType, mybir.ActivationFunctionType, mybir.AxisListType


class Shared:
    pass


def at_least(eng, s, n):
    if not isinstance(n, int) or n > 0:
        eng.wait_ge(s, n)


def after(i, c, each):
    return i * each + each * (c // SLOTS + 1)


LOOPS = (K - DEPTH) // SLOTS


def skewed(eng, step, beside=None):
    for c in range(DEPTH):
        step(0, c)
    first = NB if beside else 0
    assert first < LOOPS
    if beside:
        with eng.Fori(0, first) as i:
            beside(i)
            for c in range(DEPTH, DEPTH + SLOTS):
                step(i, c)
    with eng.Fori(first, LOOPS) as i:
        for c in range(DEPTH, DEPTH + SLOTS):
            step(i, c)
    for c in range(DEPTH, 2 * DEPTH):
        step(LOOPS, c)


def ahead(eng, work):
    for c in range(SLOTS):
        work(0, c)
    with eng.Fori(0, LOOPS - 1) as i:
        for c in range(SLOTS, 2 * SLOTS):
            work(i, c)
    for c in range(SLOTS, SLOTS + DEPTH):
        work(LOOPS - 1, c)


def item(i, c):
    return not isinstance(i, int) or 0 <= i * SLOTS + c < K


def setup_stage(nc, g, xn, xt, w, wt, a2, wm, wr, bm, br, src_h, dst_h):
    with ExitStack() as ctx:
        def sb(name, shape, dt=f32):
            return ctx.enter_context(nc.sbuf_tensor(name, shape, dt))

        def sem(name):
            return ctx.enter_context(nc.semaphore(name))

        HW = D + 2
        xts = sb("xt_sb", [P, NBP, P])
        w_sb = sb("w0_sb", [P, D])
        a_sb = sb("a_sb", [P, 2])
        wx = sb("wx", [P, HW])
        ids = sb("ids", [P, 2, EC], i32)
        hii = sb("hii", [P, 2, EC], i32)
        hi_dst = sb("hi_dst", [P, EC], bf16)
        here = sb("here", [P, 2, EC], bf16)
        er_rest = sb("er_rest", [P, 2, NBP])
        elp = sb("elp", [P, NBP, 2])
        tri = sb("tri", [P, P])
        c128 = sb("c128", [P, P])
        cnt = sb("cnt", [P, 2, NBP])
        tot = sb("tot", [P, 2, NBP])
        run = sb("run", [P, 2, NBP])
        before = sb("before", [P, NBP])
        toti = sb("toti", [P, 2, NBP], i32)
        nit = sb("nit", [P, 2, NBP])
        itend = sb("itend", [P, 2, NBP])
        dlt = sb("dlt", [P, 2, NBP])
        junk = sb("junk", [P, NBP])
        col = sb("col", [P, 4])
        past = sb("past", [P, 2, KC])
        e0f = sb("e0f", [1, 2, KC])
        low = sb("low", [P, 4])
        padrec = sb("padrec", [P, CH, RW])
        ps = [ctx.enter_context(nc.psum_tensor(f"ps_s{i}", [P, 512], f32)) for i in range(8)]

        s_ld, s_edge, s_tab, s_pad = (sem(f"su_{n}") for n in ("load", "edges", "table_stored", "pad_stored"))
        s_const, s_id, s_wx, s_wxc, s_h, s_hc, s_one, s_fix = (
            sem(f"su_{n}") for n in ("const", "ident", "wx", "wx_copied", "h", "h_copied", "one", "table_made"))
        s_low, s_lowt, s_lowm, s_lowb = (sem(f"su_{n}") for n in ("low", "low_turned", "low_least", "low_spread"))
        s_cnt, s_tot, s_col, s_it, s_itc, s_chain, s_padv = (
            sem(f"su_{n}") for n in ("counted", "totals", "columns", "items", "items_copied", "chain", "pad_made"))
        block = ctx.enter_context(nc.Block())
        groups = -(-NBP // HG)

        @block.sync
        def _(sp):
            sp.dma_start(ids[:, 0, :], dst_h.rearrange("(p c) -> p c", p=P)).then_inc(s_edge, 16)
            for to, of in ((w_sb[:, :], w), (wx[:, 0:D], wt), (a_sb[:, :], a2),
                           (xts[:, :, :], xt.rearrange("p (b n) -> p b n", n=P)),
                           (g.x[:, :, :], xn.rearrange("(b p) d -> p b d", p=P)),
                           (g.wmr[:, 0:D], wm[0:D, :]), (g.wm2[:, :], wm[D:D + FE, :]), (g.wmr[:, D:2 * D], wr),
                           (g.brow[:, 0, :], bm), (g.brow[:, 1, :], br)):
                sp.dma_start(to, of).then_inc(s_ld, 16)
            sp.dma_start(ids[:, 1, :], src_h.rearrange("(p c) -> p c", p=P)).then_inc(s_edge, 16)
            sp.wait_ge(s_fix, 1)
            sp.dma_start(g.table_d.rearrange("(b p) w -> p b w", p=P), g.table[:, :, :]).then_inc(s_tab, 16)
            sp.wait_ge(s_padv, 2)
            sp.dma_start(g.rec_d[E:E + IT, :].rearrange("(p j) w -> p j w", p=P), padrec[:, :, :]).then_inc(s_pad, 16)
            sp.wait_ge(s_tab, 16)
            sp.wait_ge(s_pad, 16)
            sp.wait_ge(s_ld, 160)

        @block.gpsimd
        def _(pool):
            pool.iota(g.iota[:, :], pattern=[[1, 512]], base=0, channel_multiplier=0, allow_small_or_imprecise_dtypes=True).then_inc(s_const, 1)
            pool.memset(g.ones[:, :], 1.0).then_inc(s_const, 1)
            pool.memset(g.onesb[:, :], 1.0).then_inc(s_const, 1)
            pool.memset(c128[:, :], float(P)).then_inc(s_const, 1)
            pool.memset(cnt[:, :, NB:NBP], 0.0).then_inc(s_const, 1)
            pool.memset(g.pos[:, :], SKIP + 1).then_inc(s_const, 1)
            pool.memset(g.ident[:, :], 0.0).then_inc(s_id, 1)
            pool.memset(tri[:, :], 0.0).then_inc(s_id, 1)
            pool.wait_ge(s_id, 2)
            pool.affine_select(out=g.ident[:, :], in_=g.ident[:, :], compare_op=ALU.not_equal, fill=1.0,
                               base=0, pattern=[[-1, P]], channel_multiplier=1).then_inc(s_id, 1)
            pool.affine_select(out=tri[:, :], in_=tri[:, :], compare_op=ALU.is_ge, fill=1.0,
                               base=0, pattern=[[-1, P]], channel_multiplier=1).then_inc(s_id, 1)
            pool.memset(padrec[:, :, 0:RW - 1], 0.0).then_inc(s_padv, 1)
            pool.memset(padrec[:, :, RW - 1:RW], float(PAD_NODE)).then_inc(s_padv, 1)
            pool.memset(g.acc[:, :, :], 0.0).then_inc(s_const, 1)
            pool.memset(g.erm[:, :, 1:2], LEAST).then_inc(s_const, 1)
            pool.memset(g.erm_parts[:, :, :, 1], 0.0).then_inc(s_const, 1)
            pool.wait_ge(s_id, 3)
            pool.tensor_copy(g.identb[:, :], g.ident[:, :]).then_inc(s_const, 1)
            pool.wait_ge(s_const, 1)
            pool.tensor_copy(g.iotab[:, :], g.iota[:, 0:P]).then_inc(s_const, 1)

        @block.scalar
        def _(act):
            act.wait_ge(s_wx, 1)
            nc.scalar.activation(wx[:, D:HW], ps[7][:, 0:2], ACT.Copy).then_inc(s_wxc, 1)
            for i in range(groups):
                nb = min(HG, NBP - HG * i)
                act.wait_ge(s_h, i + 1)
                nc.scalar.activation(g.table[:, HG * i:HG * i + nb, 0:HW],
                                     ps[i % 4][:, 0:nb * HW].rearrange("p (b w) -> p b w", w=HW), ACT.Copy).then_inc(s_hc, 1)

        @block.tensor
        def _(pe):
            pe.wait_ge(s_ld, 160)
            nc.tensor.matmul(ps[7][:, 0:2], w_sb[:, :], a_sb[:, :], start=True, stop=True).then_inc(s_wx, 1)
            pe.wait_ge(s_wxc, 1)
            for i in range(groups):
                at_least(pe, s_hc, i - 3)
                for n in range(min(HG, NBP - HG * i)):
                    h = nc.tensor.matmul(ps[i % 4][:, n * HW:(n + 1) * HW], xts[:, HG * i + n, :], wx[:, :], start=True, stop=True)
                h.then_inc(s_h, 1)
            pe.wait_ge(s_low, 1)
            pe.wait_ge(s_id, 4)
            pe.wait_ge(s_const, 2)
            nc.tensor.matmul(ps[6][0:1, 0:P], low[:, 0:1], g.ident[:, :], start=True, stop=True).then_inc(s_lowt, 1)
            pe.wait_ge(s_lowm, 1)
            nc.tensor.matmul(ps[6][:, P:P + 1], g.ones[0:1, :], low[0:1, 1:2], start=True, stop=True).then_inc(s_lowb, 1)
            pe.wait_ge(s_cnt, 1)
            nc.tensor.matmul(ps[4][:, 0:2 * NBP], g.ones[:, :], cnt[:, :, :].rearrange("p a b -> p (a b)"), start=True, stop=True)
            nc.tensor.matmul(ps[5][:, 0:NBP], tri[:, :], cnt[:, SRC, :], start=True, stop=True).then_inc(s_tot, 1)
            for a in range(2):
                pe.wait_ge(s_col, 1)
                at_least(pe, s_itc, a)
                nc.tensor.matmul(ps[0][:, 0:KC], c128[0:NB, :], past[0:NB, a, :], start=True, stop=True)
                nc.tensor.matmul(ps[1][0:1, 0:KC], col[0:NB, 2 * a + 1:2 * a + 2], past[0:NB, a, :], start=True, stop=True).then_inc(s_it, 1)

        @block.vector
        def _(dve):
            chain = [0]

            def link(ins):
                chain[0] += 1
                ins.then_inc(s_chain, 1)
                dve.wait_ge(s_chain, chain[0])

            dve.wait_ge(s_hc, groups)
            nc.vector.tensor_reduce(low[:, 0:1], g.table[:, :, D], axis=AX.X, op=ALU.min).then_inc(s_low, 1)
            link(nc.vector.tensor_copy(g.erm[:, :, 0], g.table[:, :, D + 1]))
            nc.vector.memset(g.table[:, :, D + 1:SW], 1.0).then_inc(s_one, 1)
            dve.wait_ge(s_lowt, 1)
            nc.vector.tensor_reduce(low[0:1, 1:2], ps[6][0:1, 0:P], axis=AX.X, op=ALU.min).then_inc(s_lowm, 1)
            dve.wait_ge(s_edge, 16)
            link(nc.vector.tensor_scalar(hii[:, 0, :], ids[:, 0, :], 7, None, ALU.arith_shift_right))
            link(nc.vector.tensor_copy(hi_dst[:, :], hii[:, 0, :]))
            dve.wait_ge(s_lowb, 1)
            link(nc.vector.tensor_copy(g.elmin[:, :], ps[6][:, P:P + 1]))
            link(nc.vector.tensor_scalar(g.ermin[:, :, :], g.erm[:, :, 0:1], g.elmin[:, 0:1], None, ALU.add))
            for h in range(PARTS):
                link(nc.vector.tensor_copy(g.erm_parts[:, :, h, 0], (g.erm[:, :, 0], er_rest[:, 0, :], er_rest[:, 1, :])[h]))
                if h + 1 < PARTS:
                    link(nc.vector.tensor_tensor(er_rest[:, h, :], (g.erm[:, :, 0], er_rest[:, 0, :])[h], g.erm_parts[:, :, h, 0], ALU.subtract))
            link(nc.vector.tensor_scalar(elp[:, :, 0], g.table[:, :, D], g.elmin[:, 0:1], None, ALU.subtract))
            parts = g.table[:, :, SW:TW].bitcast(bf16)
            link(nc.vector.tensor_copy(parts[:, :, 0], elp[:, :, 0]))
            link(nc.vector.tensor_tensor(elp[:, :, 1], elp[:, :, 0], parts[:, :, 0], ALU.subtract))
            dve.wait_ge(s_one, 1)
            nc.vector.tensor_copy(parts[:, :, 1], elp[:, :, 1]).then_inc(s_fix, 1)
            dve.wait_ge(s_edge, 32)
            link(nc.vector.tensor_scalar(hii[:, 1, :], ids[:, 1, :], 7, None, ALU.arith_shift_right))
            link(nc.vector.tensor_copy(g.hi[:, :], hii[:, 1, :]))
            dve.wait_ge(s_const, 11)
            with dve.Fori(0, NB) as b:
                for a, hi in enumerate((hi_dst, g.hi)):
                    dve.wait_ge(s_chain, b * 2 + chain[0] + a - 1)
                    nc.vector.tensor_scalar(here[:, a, :], hi[:, :], g.iota[:, bass.ds(b, 1)], 0.0, ALU.is_equal, ALU.add,
                                            accum_out=cnt[:, a, bass.ds(b, 1)]).then_inc(s_chain, 1)
            chain[0] += 2 * NB
            dve.wait_ge(s_chain, chain[0])
            nc.vector.tensor_copy(low[:, 2:3], cnt[:, 0, 0:1]).then_inc(s_cnt, 1)
            dve.wait_ge(s_tot, 1)
            link(nc.vector.tensor_copy(tot[:, :, :].rearrange("p a b -> p (a b)"), ps[4][:, 0:2 * NBP]))
            link(nc.vector.tensor_scalar(toti[:, :, :], tot[:, :, :], float(IT - 1), None, ALU.add))
            link(nc.vector.tensor_scalar(toti[:, :, :], toti[:, :, :], IT_BITS, None, ALU.arith_shift_right))
            link(nc.vector.tensor_copy(nit[:, :, :], toti[:, :, :]))
            for a in range(2):
                link(nc.vector.tensor_tensor_scan(itend[:, a, :], g.ones[:, 0:NBP], nit[:, a, :], 0.0, ALU.mult, ALU.add))
            link(nc.vector.tensor_tensor_scan(run[:, SRC, :], g.ones[:, 0:NBP], tot[:, SRC, :], 0.0, ALU.mult, ALU.add))
            link(nc.vector.tensor_tensor(before[:, :], run[:, SRC, :], tot[:, SRC, :], ALU.subtract))
            link(nc.vector.tensor_tensor(g.off[:, 0:NBP], before[:, :], ps[5][:, 0:NBP], ALU.add))
            link(nc.vector.scalar_tensor_tensor(dlt[:, :, :], nit[:, :, :], -float(IT), tot[:, :, :], ALU.mult, ALU.add))
            for a in range(2):
                for i, t in enumerate((itend, dlt)):
                    link(nc.vector.scalar_tensor_tensor(junk[:, :], t[:, a, :], 1.0, g.ident[:, 0:NBP], ALU.mult, ALU.mult,
                                                        accum_out=col[:, 2 * a + i:2 * a + i + 1]))
                link(nc.vector.tensor_scalar(past[:, a, :], g.iota[:, 0:KC], col[:, 2 * a:2 * a + 1], None, ALU.is_ge))
            nc.vector.tensor_copy(low[:, 3:4], col[:, 0:1]).then_inc(s_col, 1)
            for a, cap in ((DST, EP - IT), (SRC, E)):
                dve.wait_ge(s_it, a + 1)
                link(nc.vector.tensor_copy(g.b128[:, a, :], ps[0][:, 0:KC]))
                link(nc.vector.tensor_scalar(g.bt[:, a, :], g.b128[0:1, a, :], 1.0 / P, None, ALU.mult))
                link(nc.vector.scalar_tensor_tensor(e0f[:, a, :], g.iota[0:1, 0:KC], float(IT), ps[1][0:1, 0:KC], ALU.mult, ALU.add))
                nc.vector.tensor_scalar(g.e0t[:, a, :], e0f[:, a, :], float(cap), None, ALU.min).then_inc(s_itc, 1)


def first_layer_stage(nc, g, meta_h):
    with ExitStack() as ctx:
        def sb(name, shape, dt=f32):
            return ctx.enter_context(nc.sbuf_tensor(name, shape, dt))

        def sem(name):
            return ctx.enter_context(nc.semaphore(name))

        def bank(name, dt=f32):
            return ctx.enter_context(nc.psum_tensor(name, [P, CH * P], dt))

        meta = sb("meta1", [P, SLOTS, CH, 2], i32)
        rows = sb("rows", [P, SLOTS, CH, TW])
        rel = sb("rel1", [P, 2, CH])
        hot = sb("hot1", [P, DEPTH, CH, P], bf16)
        apart = sb("apart", [P, CH, P], bf16)
        hot_t = sb("hot_t1", [P, 2, CH * P], bf16)
        seen = sb("seen", [P, 2, CH * P], bf16)
        wgt = sb("wgt", [P, 2, CH, P])
        mx = sb("mx", [P, 2, 6])
        sc = sb("sc", [P, 2, 4, CH])
        fade = sb("fade", [P, DEPTH, 1])
        here = sb("here1", [P, EC], bf16)
        scan = sb("scan", [P, EC])
        posi = sb("posi", [P, EC], i32)
        ps_t = [bank(f"ps_t{i}", bf16) for i in range(2)]
        ps_x = [bank(f"ps_x{i}") for i in range(2)]
        ps_o = [bank(f"ps_o{i}") for i in range(2)]
        ps_e = [bank(f"ps_e{i}") for i in range(2)]

        meta_in = [sem(f"meta_in{i}") for i in range(SLOTS)]
        gathered = [sem(f"gathered{i}") for i in range(SLOTS)]
        (s_rel, s_hot, s_turned, s_hot_t, s_spread, s_max, s_sum, s_leaky, s_m, s_grown, s_kept, s_picked, s_z, s_lz,
         s_q, s_p, s_wgt, s_out, s_fade, s_acc, s_pass, s_here, s_scan, s_pos, s_posi, s_stored, s_apart, s_m1, s_m2, s_short) = (
            sem(f"l1_{n}") for n in ("rel", "hot", "turned", "hot_t", "spread", "max", "sum", "leaky", "m",
                                     "grown", "kept", "picked", "z", "lz", "q", "p", "wgt", "out", "fade", "acc", "pass",
                                     "here", "scan", "pos", "posi", "stored", "apart", "m1", "m2", "short"))
        block = ctx.enter_context(nc.Block())

        @block.sync
        def _(sp):
            def load(i, c):
                s, k = c % SLOTS, i * SLOTS + c
                e0 = sp.value_load(g.e0t[0:1, DST, bass.ds(k, 1)], min_val=0, max_val=EP - IT)
                at_least(sp, s_rel, k - SLOTS + 1)
                at_least(sp, s_out, k - SLOTS + 1)
                sp.dma_start(meta[:, s, :, :], meta_h[bass.ds(e0, IT), :].rearrange("(p j) w -> p j w", p=P)).then_inc(meta_in[s], 16)

            ahead(sp, load)
            load(LOOPS - 1, SLOTS + DEPTH)
            sp.wait_ge(s_posi, 1)
            sp.dma_start(g.pos_d.rearrange("(p c) -> p c", p=P), posi[:, :]).then_inc(s_stored, 16)
            sp.wait_ge(s_stored, 16)

        @block.gpsimd
        def _(pool):
            def gather(i, c):
                s, k = c % SLOTS, i * SLOTS + c
                pool.wait_ge(meta_in[s], after(i, c, 16))
                at_least(pool, s_out, k - SLOTS + 1)
                pool.sem_inc(s_pass, 1)
                for j in range(CH):
                    pool.indirect_dma_start(out=rows[:, s, j, :], out_offset=None, in_=g.table_d,
                                            in_offset=bass.IndirectOffsetOnAxis(ap=meta[:, s, j, 0:1], axis=0)).then_inc(gathered[s], 16)

            ahead(pool, gather)

        @block.scalar
        def _(act):
            def mark(i, c):
                k = i * SLOTS + c
                act.wait_ge(s_rel, k + 1)
                at_least(act, s_hot, k)
                for j in range(CH):
                    apart_j = nc.scalar.activation(apart[:, j, :], g.iotab[:, :], ACT.Abs, bias=rel[:, c % 2, j:j + 1])
                apart_j.then_inc(s_apart, 1)
                act.wait_ge(s_apart, k + 1)
                at_least(act, s_wgt, k - 2)
                at_least(act, s_turned, k - 2)
                nc.scalar.activation(hot[:, c % DEPTH, :, :], apart[:, :, :], ACT.Relu, scale=-1.0, bias=1.0).then_inc(s_hot, 1)

            def step(i, c):
                k = i * SLOTS + c
                if isinstance(k, int) and k == 0:
                    mark(i, c)
                if item(i, c):
                    act.wait_ge(s_turned, k + 1)
                    at_least(act, s_picked, k - 1)
                    at_least(act, s_max, k - 1)
                    nc.scalar.activation(hot_t[:, c % 2, :], ps_t[c % 2][:, :], ACT.Copy).then_inc(s_hot_t, 1)
                if item(i, c - 2):
                    act.wait_ge(s_q, k - 1)
                    at_least(act, s_wgt, k - 3)
                    nc.scalar.activation(sc[:, c % 2, 3, :], sc[:, c % 2, 2, :], ACT.Exp).then_inc(s_p, 1)
                if item(i, c - 1):
                    act.wait_ge(s_grown, k)
                    at_least(act, s_acc, k - 3)
                    nc.scalar.activation(fade[:, (c - 1) % DEPTH, :], mx[:, (c - 1) % 2, 5:6], ACT.Exp).then_inc(s_fade, 1)
                if item(i, c + 1):
                    mark(i, c + 1)

            skewed(act, step)

        @block.tensor
        def _(pe):
            def step(i, c):
                k = i * SLOTS + c
                u, v = c % 2, (c - 1) % 2
                b = pe.value_load(g.bt[0:1, DST, bass.ds(k - 1, 1)], min_val=0, max_val=NB) if item(i, c - 1) else None
                if item(i, c):
                    pe.wait_ge(s_hot, k + 1)
                    at_least(pe, s_hot_t, k - 1)
                    for j in range(CH):
                        mm = nc.tensor.transpose(ps_t[u][:, j * P:(j + 1) * P], hot[:, c % DEPTH, j, :], g.identb[:, :])
                    mm.then_inc(s_turned, 1)
                if item(i, c):
                    pe.wait_ge(gathered[c % SLOTS], after(i, c, 16 * CH))
                    at_least(pe, s_max, k - 1)
                    for j in range(CH):
                        parts = rows[:, c % SLOTS, j, SW:TW].bitcast(bf16)
                        for h in range(2):
                            mm = nc.tensor.matmul(ps_x[u][:, j * P:(j + 1) * P], parts[:, h:h + 1].to_broadcast([P, P]), g.identb[:, :],
                                                  start=h == 0, stop=h == 1)
                    mm.then_inc(s_spread, 1)
                if b is not None:
                    pe.wait_ge(s_m2, k)
                    pe.wait_ge(s_hot_t, k)
                    at_least(pe, s_q, k - 2)
                    for j in range(CH):
                        for h in range(PARTS):
                            mm = nc.tensor.matmul(ps_e[v][:, 2 * j:2 * j + 2], hot_t[:, v, j * P:(j + 1) * P], g.erm_parts[:, bass.ds(b, 1), h, :],
                                                  start=h == 0, stop=h == PARTS - 1)
                    mm.then_inc(s_picked, 1)
                if item(i, c - 2):
                    pe.wait_ge(s_wgt, k - 1)
                    at_least(pe, s_acc, k - 3)
                    for j in range(CH):
                        mm = nc.tensor.matmul(ps_o[u][:, 0:SW], wgt[:, u, j, :], rows[:, (c - 2) % SLOTS, j, 0:SW], start=j == 0, stop=j == CH - 1)
                    mm.then_inc(s_out, 1)

            skewed(pe, step)

        @block.vector
        def _(dve):
            loaded = {}

            def block_of(i, c):
                if not item(i, c):
                    return None
                if (id(i), c) not in loaded:
                    loaded[id(i), c] = load_block(i, c)
                return loaded[id(i), c]

            def load_block(i, c):
                return bass.ds(dve.value_load(g.bt[0:1, DST, bass.ds(i * SLOTS + c, 1)], min_val=0, max_val=NB), 1)

            def place(b):
                at_least(dve, s_pos, b)
                nc.vector.tensor_scalar(here[:, :], g.hi[:, :], g.iota[:, bass.ds(b, 1)], None, ALU.is_equal).then_inc(s_here, 1)
                dve.wait_ge(s_here, b + 1)
                nc.vector.tensor_tensor_scan(scan[:, :], g.onesb[:, :], here[:, :], g.off[:, bass.ds(b, 1)], ALU.mult, ALU.add).then_inc(s_scan, 1)
                dve.wait_ge(s_scan, b + 1)
                dve.sem_inc(s_pass, 1)
                nc.vector.copy_predicated(g.pos[:, :], here[:, :].bitcast(mybir.dt.uint16), scan[:, :]).then_inc(s_pos, 1)

            def within(i, c):
                k = i * SLOTS + c
                dve.wait_ge(meta_in[c % SLOTS], after(i, c, 16))
                at_least(dve, s_hot, k - 1)
                nc.vector.tensor_scalar(rel[:, c % 2, :], meta[:, c % SLOTS, :, 1], -1.0, g.b128[:, DST, bass.ds(k, 1)], ALU.mult, ALU.add).then_inc(s_rel, 1)

            def step(i, c):
                k = i * SLOTS + c
                u, v = c % 2, (c - 1) % 2
                s2 = (c - 2) % SLOTS
                b1, b3 = block_of(i, c - 1), block_of(i, c - 3)
                one, two = item(i, c - 1), item(i, c - 2)
                er_m = ps_e[u][:, 0:2 * CH].rearrange("p (j w) -> p j w", w=2)
                if isinstance(k, int) and k == 0:
                    within(i, c)
                if one:
                    dve.wait_ge(s_spread, k)
                    dve.wait_ge(s_hot_t, k)
                    at_least(dve, s_max, k - 2)
                    dve.sem_inc(s_pass, 1)
                    nc.vector.tensor_tensor_reduce(seen[:, v, :], ps_x[v][:, :], hot_t[:, v, :], 1.0, 0.0, ALU.mult, ALU.max,
                                                   mx[:, v, 0:1]).then_inc(s_max, 1)
                if two:
                    dve.wait_ge(s_picked, k - 1)
                    nc.vector.tensor_tensor(sc[:, u, 0, :], rows[:, s2, :, D], er_m[:, :, 0], ALU.add).then_inc(s_z, 1)
                if one:
                    dve.wait_ge(s_max, k)
                    nc.vector.tensor_tensor(mx[:, v, 1:2], mx[:, v, 0:1], g.ermin[:, b1, 0], ALU.add).then_inc(s_sum, 1)
                if two:
                    dve.wait_ge(s_z, k - 1)
                    nc.vector.scalar_tensor_tensor(sc[:, u, 1, :], sc[:, u, 0, :], SLOPE, sc[:, u, 0, :], ALU.mult, ALU.max).then_inc(s_lz, 1)
                if one:
                    dve.wait_ge(s_sum, k)
                    nc.vector.scalar_tensor_tensor(mx[:, v, 2:3], mx[:, v, 1:2], SLOPE, mx[:, v, 1:2], ALU.mult, ALU.max).then_inc(s_leaky, 1)
                if two:
                    dve.wait_ge(s_lz, k - 1)
                    at_least(dve, s_p, k - 3)
                    nc.vector.tensor_tensor(sc[:, u, 2, :], sc[:, u, 1, :], er_m[:, :, 1], ALU.subtract).then_inc(s_q, 1)
                if one:
                    dve.wait_ge(s_leaky, k)
                    at_least(dve, s_kept, k - 1)
                    nc.vector.tensor_tensor(mx[:, v, 3:4], mx[:, v, 2:3], g.erm[:, b1, 1], ALU.max).then_inc(s_m, 1)
                if one:
                    dve.wait_ge(s_m, k)
                    at_least(dve, s_picked, k - 1)
                    m_parts = g.erm_parts[:, b1, :, 1]
                    nc.vector.tensor_scalar(m_parts[:, :, 0], mx[:, v, 3:4], 0.0, None, ALU.add).then_inc(s_m1, 1)
                if item(i, c + 1):
                    within(i, c + 1)
                if one:
                    dve.wait_ge(s_m1, k)
                    nc.vector.tensor_tensor(m_parts[:, :, 1], mx[:, v, 3:4], m_parts[:, :, 0], ALU.subtract).then_inc(s_m2, 1)
                if b3 is not None:
                    dve.wait_ge(s_out, k - 2)
                    dve.wait_ge(s_fade, k - 2)
                    at_least(dve, s_acc, k - 3)
                    nc.vector.scalar_tensor_tensor(g.acc[:, b3, :], g.acc[:, b3, :], fade[:, c % DEPTH, :],
                                                   ps_o[v][:, 0:SW].unsqueeze(1), ALU.mult, ALU.add).then_inc(s_acc, 1)
                if one:
                    dve.wait_ge(s_m2, k)
                    nc.vector.tensor_tensor(mx[:, v, 4:5], m_parts[:, :, 0], m_parts[:, :, 1], ALU.add).then_inc(s_short, 1)
                    dve.wait_ge(s_short, k)
                    at_least(dve, s_fade, k - 2)
                    nc.vector.tensor_tensor(mx[:, v, 5:6], g.erm[:, b1, 1], mx[:, v, 4:5], ALU.subtract).then_inc(s_grown, 1)
                    dve.wait_ge(s_grown, k)
                    nc.vector.tensor_scalar(g.erm[:, b1, 1], mx[:, v, 4:5], 0.0, None, ALU.add).then_inc(s_kept, 1)
                if two:
                    dve.wait_ge(s_p, k - 1)
                    at_least(dve, s_out, k - 3)
                    nc.vector.scalar_tensor_tensor(wgt[:, u, :, :], sc[:, u, 3, :].unsqueeze(2).to_broadcast([P, CH, P]), MOST,
                                                   hot[:, (c - 2) % DEPTH, :, :], ALU.min, ALU.mult).then_inc(s_wgt, 1)

            skewed(dve, step, beside=place)
            dve.wait_ge(s_pos, NB)
            nc.vector.tensor_scalar(posi[:, :], g.pos[:, :], -1.0, None, ALU.add).then_inc(s_posi, 1)


def norm_stage(nc, g, val, name, first):
    with ExitStack() as ctx:
        tmp = ctx.enter_context(nc.sbuf_tensor(f"{name}_tmp", [P, NB, D], f32))
        st = ctx.enter_context(nc.sbuf_tensor(f"{name}_st", [P, 5, NB], f32))
        s_sq, s_root, s_v, s_var, s_centred = (
            ctx.enter_context(nc.semaphore(f"{name}_{n}")) for n in ("sq", "root", "v", "var", "centred"))
        block = ctx.enter_context(nc.Block())

        @block.scalar
        def _(act):
            act.wait_ge(s_centred, 1)
            nc.scalar.activation(tmp[:, :, :], val[:, 0:NB, :], ACT.Square).then_inc(s_sq, 1)
            act.wait_ge(s_var, 1)
            nc.scalar.activation(st[:, 3, :], st[:, 2, :], ACT.Sqrt).then_inc(s_root, 1)

        @block.vector
        def _(dve):
            chain = [0]

            def link(ins):
                chain[0] += 1
                ins.then_inc(s_v, 1)
                dve.wait_ge(s_v, chain[0])

            def spread(i):
                return st[:, i, :].unsqueeze(2).to_broadcast([P, NB, D])

            v = val[:, 0:NB, :]
            if first:
                link(nc.vector.tensor_scalar(st[:, 0, :], g.acc[:, 0:NB, SW - 1], 1e-38, None, ALU.max))
                link(nc.vector.reciprocal(st[:, 1, :], st[:, 0, :]))
                link(nc.vector.tensor_tensor(tmp[:, :, :], g.acc[:, 0:NB, 0:D], spread(1), ALU.mult))
                link(nc.vector.tensor_tensor(v, v, tmp[:, :, :], ALU.add))
            link(nc.vector.tensor_reduce(st[:, 0, :], v, axis=AX.X, op=ALU.add))
            link(nc.vector.tensor_scalar(st[:, 1, :], st[:, 0, :], 1.0 / D, None, ALU.mult))
            nc.vector.tensor_tensor(v, v, spread(1), ALU.subtract).then_inc(s_centred, 1)
            dve.wait_ge(s_sq, 1)
            link(nc.vector.tensor_reduce(st[:, 0, :], tmp[:, :, :], axis=AX.X, op=ALU.add))
            nc.vector.tensor_scalar(st[:, 2, :], st[:, 0, :], 1.0 / D, EPS, ALU.mult, ALU.add).then_inc(s_var, 1)
            dve.wait_ge(s_root, 1)
            link(nc.vector.reciprocal(st[:, 4, :], st[:, 3, :]))
            nc.vector.tensor_tensor(v, v, spread(4), ALU.mult)


def project_stage(nc, g):
    with ExitStack() as ctx:
        def sem(name):
            return ctx.enter_context(nc.semaphore(name))

        turned = ctx.enter_context(nc.sbuf_tensor("turned", [P, 2, P], f32))
        rest = ctx.enter_context(nc.sbuf_tensor("rest", [P, 2, P], f32))
        ps_t = [ctx.enter_context(nc.psum_tensor(f"ps_f{i}", [P, 512], f32)) for i in range(2)]
        ps_y = [ctx.enter_context(nc.psum_tensor(f"ps_y{i}", [P, 512], f32)) for i in range(2)]
        ps_r = [ctx.enter_context(nc.psum_tensor(f"ps_r{i}", [P, 512], f32)) for i in range(2)]
        s_half, s_bias, s_turned, s_cp, s_y, s_a, s_b, s_r, s_c, s_sum = (
            sem(f"pj_{n}") for n in ("halved", "bias", "turned", "copied", "y", "part_a", "part_b", "rest", "part_c", "sum"))
        block = ctx.enter_context(nc.Block())

        @block.scalar
        def _(act):
            nc.scalar.activation(g.wmr[:, 0:D], g.wmr[:, 0:D], ACT.Copy, scale=0.5).then_inc(s_half, 1)
            nc.scalar.activation(g.wm2[:, :], g.wm2[:, :], ACT.Copy, scale=0.5).then_inc(s_half, 1)
            for b in range(NB + 1):
                u, v = b % 2, (b - 1) % 2
                if b < NB:
                    act.wait_ge(s_turned, b + 1)
                    at_least(act, s_y, b - 1)
                    nc.scalar.activation(turned[:, u, :], ps_t[u][:, 0:P], ACT.Copy).then_inc(s_cp, 1)
                if b > 0:
                    act.wait_ge(s_y, b)
                    nc.scalar.activation(g.parts[:, b - 1, 0, :], ps_y[v][:, 0:D], ACT.Copy).then_inc(s_a, 1)
                    act.wait_ge(s_r, b)
                    nc.scalar.activation(g.parts[:, b - 1, 1, :], rest[:, v, :], ACT.Copy).then_inc(s_b, 1)

        @block.tensor
        def _(pe):
            pe.wait_ge(s_half, 2)
            pe.wait_ge(s_bias, 1)
            for b in range(NB + 1):
                u, v = b % 2, (b - 1) % 2
                if b < NB:
                    at_least(pe, s_cp, b - 1)
                    nc.tensor.transpose(ps_t[u][:, 0:P], g.x[:, b, :], g.ident[:, :]).then_inc(s_turned, 1)
                if b > 0:
                    pe.wait_ge(s_cp, b)
                    at_least(pe, s_sum, b - 2)
                    at_least(pe, s_c, b - 2)
                    nc.tensor.matmul(ps_y[v][:, 0:D], turned[:, v, :], g.wmr[:, 0:D], start=True, stop=True)
                    nc.tensor.matmul(ps_r[v][:, 0:D], turned[:, v, :], g.wmr[:, D:2 * D], start=True, stop=False)
                    nc.tensor.matmul(ps_r[v][:, 0:D], g.ones[0:1, :], g.brow[:, 2, :], start=False, stop=True).then_inc(s_y, 1)

        @block.vector
        def _(dve):
            nc.vector.scalar_tensor_tensor(g.brow[:, 2, :], g.brow[:, 0, :], 0.5, g.brow[:, 1, :], ALU.mult, ALU.add).then_inc(s_bias, 1)
            for b in range(NB):
                u = b % 2
                dve.wait_ge(s_y, b + 1)
                nc.vector.tensor_tensor(g.sums[:, b, :], g.x[:, b, :], ps_r[u][:, 0:D], ALU.add).then_inc(s_sum, 1)
                dve.wait_ge(s_a, b + 1)
                at_least(dve, s_c, b - 1)
                nc.vector.tensor_tensor(rest[:, u, :], ps_y[u][:, 0:D], g.parts[:, b, 0, :], ALU.subtract).then_inc(s_r, 1)
                dve.wait_ge(s_b, b + 1)
                nc.vector.tensor_tensor(g.parts[:, b, 2, :], rest[:, u, :], g.parts[:, b, 1, :], ALU.subtract).then_inc(s_c, 1)
            nc.vector.memset(g.parts[:, NB, :, :], 0.0)
            nc.vector.memset(g.sums[:, NB, :], 0.0)


def record_stage(nc, g, meta_h, feat_h):
    with ExitStack() as ctx:
        def sb(name, shape, dt=f32):
            return ctx.enter_context(nc.sbuf_tensor(name, shape, dt))

        def sem(name):
            return ctx.enter_context(nc.semaphore(name))

        meta = sb("meta2", [P, SLOTS, CH, 2], i32)
        posn = sb("posn", [P, SLOTS, CH], i32)
        feat = sb("feat", [FE, SLOTS, IT])
        rec = sb("rec2", [P, SLOTS, CH, RW])
        rel = sb("rel2", [P, 2, CH])
        far = sb("far", [P, 2, 2, CH])
        hot = sb("hot2", [P, 2, CH, P], bf16)
        hot_t = sb("hot_t2", [P, 2, CH * P], bf16)
        to = sb("to", [P, SLOTS, CH], i32)
        ps_t = [ctx.enter_context(nc.psum_tensor(f"ps_h{i}", [P, 512], bf16)) for i in range(2)]
        ps_g = [ctx.enter_context(nc.psum_tensor(f"ps_g{i}", [P, 512], f32)) for i in range(2)]
        edge_in = [sem(f"edge_in{i}") for i in range(SLOTS)]
        scattered = [sem(f"scattered{i}") for i in range(SLOTS)]
        (s_rel, s_hot, s_src, s_far, s_out_of, s_to, s_turned, s_hot_t, s_got, s_rec, s_pass) = (
            sem(f"rc_{n}") for n in ("rel", "hot", "src", "far", "outside", "to", "turned", "hot_t", "got", "rec", "pass"))
        block = ctx.enter_context(nc.Block())

        @block.sync
        def _(sp):
            def load(i, c):
                s, k = c % SLOTS, i * SLOTS + c
                e0 = sp.value_load(g.e0t[0:1, DST, bass.ds(k, 1)], min_val=0, max_val=EP - IT)
                if not isinstance(i, int) or c >= SLOTS:
                    sp.wait_ge(scattered[s], after(i, c - SLOTS, 16 * CH))
                sp.dma_start(meta[:, s, :, :], meta_h[bass.ds(e0, IT), :].rearrange("(p j) w -> p j w", p=P)).then_inc(edge_in[s], 16)
                sp.dma_start(posn[:, s, :], g.pos_d[bass.ds(e0, IT)].rearrange("(p j) -> p j", p=P)).then_inc(edge_in[s], 16)
                sp.dma_start(feat[:, s, :], feat_h[:, bass.ds(e0, IT)]).then_inc(edge_in[s], 16)

            ahead(sp, load)
            for s in range(SLOTS):
                sp.wait_ge(scattered[s], 16 * CH * len(range(s, K, SLOTS)))

        @block.gpsimd
        def _(pool):
            def scatter(i, c):
                s, k = c % SLOTS, i * SLOTS + c
                pool.wait_ge(s_to, k + 1)
                pool.wait_ge(s_src, k + 1)
                pool.wait_ge(s_rec, k + 1)
                pool.sem_inc(s_pass, 1)
                for j in range(CH):
                    pool.indirect_dma_start(out=g.rec_d, out_offset=bass.IndirectOffsetOnAxis(ap=to[:, s, j:j + 1], axis=0),
                                            in_=rec[:, s, j, :], in_offset=None,
                                            bounds_check=E - 1, oob_is_err=False).then_inc(scattered[s], 16)

            ahead(pool, scatter)

        @block.scalar
        def _(act):
            def step(i, c):
                k = i * SLOTS + c
                if item(i, c):
                    act.wait_ge(s_turned, k + 1)
                    at_least(act, s_got, k - 1)
                    nc.scalar.activation(hot_t[:, c % 2, :], ps_t[c % 2][:, :], ACT.Copy).then_inc(s_hot_t, 1)
                if item(i, c - 1):
                    act.wait_ge(s_got, k)
                    act.wait_ge(edge_in[(c - 1) % SLOTS], after(i, c - 1, 48))
                    nc.scalar.activation(rec[:, (c - 1) % SLOTS, :, 0:D], ps_g[(c - 1) % 2][:, :].rearrange("p (j n) -> p j n", n=P),
                                         ACT.Copy).then_inc(s_rec, 1)

            skewed(act, step)

        @block.tensor
        def _(pe):
            def step(i, c):
                k = i * SLOTS + c
                u, v = c % 2, (c - 1) % 2
                b = pe.value_load(g.bt[0:1, DST, bass.ds(k - 1, 1)], min_val=0, max_val=NB) if item(i, c - 1) else None
                if item(i, c):
                    pe.wait_ge(s_hot, k + 1)
                    at_least(pe, s_hot_t, k - 1)
                    for j in range(CH):
                        mm = nc.tensor.transpose(ps_t[u][:, j * P:(j + 1) * P], hot[:, u, j, :], g.identb[:, :])
                    mm.then_inc(s_turned, 1)
                if b is not None:
                    pe.wait_ge(s_hot_t, k)
                    at_least(pe, s_rec, k - 2)
                    for j in range(CH):
                        to_j = ps_g[v][:, j * P:(j + 1) * P]
                        for h in range(PARTS):
                            nc.tensor.matmul(to_j, hot_t[:, v, j * P:(j + 1) * P], g.parts[:, bass.ds(b, 1), h, :], start=h == 0, stop=False)
                        mm = nc.tensor.matmul(to_j, feat[:, (c - 1) % SLOTS, j:IT:CH], g.wm2[:, :], start=False, stop=True)
                    mm.then_inc(s_got, 1)

            skewed(pe, step)

        @block.vector
        def _(dve):
            def step(i, c):
                k = i * SLOTS + c
                if not item(i, c):
                    return
                u, s = c % 2, c % SLOTS
                dve.wait_ge(edge_in[s], after(i, c, 48))
                at_least(dve, s_hot, k - 1)
                nc.vector.tensor_scalar(rel[:, u, :], meta[:, s, :, 1], g.b128[:, DST, bass.ds(k, 1)], None, ALU.subtract).then_inc(s_rel, 1)
                nc.vector.tensor_copy(rec[:, s, :, RW - 1], meta[:, s, :, 0]).then_inc(s_src, 1)
                dve.wait_ge(s_rel, k + 1)
                at_least(dve, s_to, k - 1)
                nc.vector.scalar_tensor_tensor(far[:, u, 0, :], rel[:, u, :], -(P - 1.0), rel[:, u, :], ALU.add, ALU.mult).then_inc(s_far, 1)
                at_least(dve, s_turned, k - 1)
                for j in range(CH):
                    hot_j = nc.vector.tensor_scalar(hot[:, u, j, :], g.iotab[:, :], rel[:, u, j:j + 1], None, ALU.is_equal)
                hot_j.then_inc(s_hot, 1)
                dve.wait_ge(s_far, k + 1)
                nc.vector.tensor_scalar(far[:, u, 1, :], far[:, u, 0, :], 0.0, SKIP, ALU.is_gt, ALU.mult).then_inc(s_out_of, 1)
                dve.wait_ge(s_out_of, k + 1)
                nc.vector.tensor_tensor(to[:, s, :], posn[:, s, :], far[:, u, 1, :], ALU.add).then_inc(s_to, 1)

            skewed(dve, step)


def sum_stage(nc, g):
    with ExitStack() as ctx:
        def sb(name, shape, dt=f32):
            return ctx.enter_context(nc.sbuf_tensor(name, shape, dt))

        def sem(name):
            return ctx.enter_context(nc.semaphore(name))

        rec = sb("rec3", [P, SLOTS, CH, RW])
        rel = sb("rel3", [P, 2, CH])
        hot = sb("hot3", [P, 2, CH, P])
        ps_a = [ctx.enter_context(nc.psum_tensor(f"ps_a{i}", [P, 512], f32)) for i in range(2)]
        rec_in = [sem(f"rec_in{i}") for i in range(SLOTS)]
        s_rel, s_hot, s_sum, s_acc = (sem(f"sm_{n}") for n in ("rel", "hot", "sum", "acc"))
        block = ctx.enter_context(nc.Block())

        @block.sync
        def _(sp):
            def load(i, c):
                s, k = c % SLOTS, i * SLOTS + c
                e0 = sp.value_load(g.e0t[0:1, SRC, bass.ds(k, 1)], min_val=0, max_val=E)
                at_least(sp, s_sum, k - SLOTS + 1)
                sp.dma_start(rec[:, s, :, :], g.rec_d[bass.ds(e0, IT), :].rearrange("(p j) w -> p j w", p=P)).then_inc(rec_in[s], 16)

            ahead(sp, load)

        @block.tensor
        def _(pe):
            def step(i, c):
                k = i * SLOTS + c
                if not item(i, c):
                    return
                u, s = c % 2, c % SLOTS
                pe.wait_ge(s_hot, k + 1)
                at_least(pe, s_acc, k - 1)
                for j in range(CH):
                    mm = nc.tensor.matmul(ps_a[u][:, 0:D], hot[:, u, j, :], rec[:, s, j, 0:D], start=j == 0, stop=j == CH - 1)
                mm.then_inc(s_sum, 1)

            skewed(pe, step)

        @block.vector
        def _(dve):
            def step(i, c):
                k = i * SLOTS + c
                u, v, s = c % 2, (c - 1) % 2, c % SLOTS
                b = bass.ds(dve.value_load(g.bt[0:1, SRC, bass.ds(k - 1, 1)], min_val=0, max_val=NB), 1) if item(i, c - 1) else None
                if item(i, c):
                    dve.wait_ge(rec_in[s], after(i, c, 16))
                    at_least(dve, s_hot, k - 1)
                    nc.vector.tensor_scalar(rel[:, u, :], rec[:, s, :, RW - 1], g.b128[:, SRC, bass.ds(k, 1)], None, ALU.subtract).then_inc(s_rel, 1)
                    dve.wait_ge(s_rel, k + 1)
                    at_least(dve, s_sum, k - 1)
                    nc.vector.tensor_tensor(hot[:, u, :, :], g.iota[:, 0:P].unsqueeze(1).to_broadcast([P, CH, P]),
                                            rel[:, u, :].unsqueeze(2).to_broadcast([P, CH, P]), ALU.is_equal).then_inc(s_hot, 1)
                if b is not None:
                    dve.wait_ge(s_sum, k)
                    at_least(dve, s_acc, k - 1)
                    nc.vector.tensor_tensor(g.sums[:, b, :], g.sums[:, b, :], ps_a[v][:, 0:D].unsqueeze(1), ALU.add).then_inc(s_acc, 1)

            skewed(dve, step)


def gnn_two_layers(nc, xn, xt, w, wt, a2, wm, wr, bm, br, src_h, dst_h, meta_h, feat_h, out):
    with ExitStack() as ctx:
        def sb(name, shape, dt=f32):
            return ctx.enter_context(nc.sbuf_tensor(name, shape, dt))

        g = Shared()
        g.table_d = nc.dram_tensor("node_table", (NP, TW), f32).ap()
        g.pos_d = nc.dram_tensor("edge_position", (EP,), i32).ap()
        g.rec_d = nc.dram_tensor("records", (E + IT, RW), f32).ap()
        g.x = sb("x", [P, NBP, D])
        first = sb("first", [P, NBP, PARTS * D // 2])
        g.acc = first[:, :, 0:SW]
        g.parts = first[:, :, :].bitcast(bf16).rearrange("p b (h d) -> p b h d", h=PARTS)
        second = sb("second", [P, NBP, TW])
        g.table = second[:, :, :]
        g.sums = second[:, :, 0:D]
        g.erm = sb("erm", [P, NBP, 2])
        g.erm_parts = sb("erm_parts", [P, NBP, PARTS, 2], bf16)
        g.ermin = sb("ermin", [P, NBP, 1])
        g.elmin = sb("elmin", [P, 1])
        g.ident = sb("ident", [P, P])
        g.identb = sb("identb", [P, P], bf16)
        g.ones = sb("ones", [P, P])
        g.iota = sb("iota", [P, 512])
        g.iotab = sb("iotab", [P, P], bf16)
        g.wmr = sb("wmr", [P, 2 * D])
        g.wm2 = sb("wm2", [FE, D])
        g.brow = sb("brow", [1, 3, D])
        g.b128 = sb("b128", [P, 2, KC])
        g.e0t = sb("e0t", [1, 2, KC], i32)
        g.bt = sb("bt", [1, 2, KC], i32)
        with ExitStack() as early:
            g.hi = early.enter_context(nc.sbuf_tensor("hi_src", [P, EC], bf16))
            g.onesb = early.enter_context(nc.sbuf_tensor("onesb", [P, EC], bf16))
            g.pos = early.enter_context(nc.sbuf_tensor("pos", [P, EC], f32))
            g.off = early.enter_context(nc.sbuf_tensor("off", [P, NBP], f32))
            setup_stage(nc, g, xn, xt, w, wt, a2, wm, wr, bm, br, src_h, dst_h)
            first_layer_stage(nc, g, meta_h)
        norm_stage(nc, g, g.x, "n1", True)
        project_stage(nc, g)
        record_stage(nc, g, meta_h, feat_h)
        sum_stage(nc, g)
        norm_stage(nc, g, g.sums, "n2", False)
        s_out = ctx.enter_context(nc.semaphore("stored"))
        block = ctx.enter_context(nc.Block())

        @block.sync
        def _(sp):
            sp.dma_start(out[0:(NB - 1) * P, :].rearrange("(b p) d -> p b d", p=P), g.sums[:, 0:NB - 1, :]).then_inc(s_out, 16)
            sp.dma_start(out[(NB - 1) * P:N, :], g.sums[0:LAST, NB - 1, :]).then_inc(s_out, 16)
            sp.wait_ge(s_out, 32)


def kernel(x, src, dst, edge_attr_32, edge_attr_32_n2, L0_gnn_W, L0_gnn_a_left, L0_gnn_a_right,
           L1_gnn_Wm, L1_gnn_bm, L1_gnn_Wr, L1_gnn_br):
    import numpy as np
    import concourse.bacc as bacc
    from concourse.bass_utils import run_bass_kernel_spmd

    def rows(a, n, fill):
        a = np.asarray(a)
        return np.concatenate([a, np.full((n - len(a),) + a.shape[1:], fill, a.dtype)])

    xp = rows(x, NP, 0)
    sp, dp = rows(src, EP, PAD_NODE), rows(dst, EP, PAD_NODE)
    ins = {
        "xn": xp, "xt": np.ascontiguousarray(xp.T),
        "w": np.asarray(L0_gnn_W), "wt": np.ascontiguousarray(np.asarray(L0_gnn_W).T),
        "a2": np.ascontiguousarray(np.concatenate([np.asarray(L0_gnn_a_left), np.asarray(L0_gnn_a_right)]).T),
        "wm": np.asarray(L1_gnn_Wm), "wr": np.asarray(L1_gnn_Wr),
        "bm": np.asarray(L1_gnn_bm)[None, :], "br": np.asarray(L1_gnn_br)[None, :],
        "src_h": sp, "dst_h": dp, "meta_h": np.stack([sp, dp], axis=1),
        "feat_h": np.ascontiguousarray(rows(np.concatenate([np.asarray(edge_attr_32), np.asarray(edge_attr_32_n2)], axis=1), EP, 0).T),
    }
    nc = bacc.Bacc("TRN2", target_bir_lowering=False, num_devices=1)
    args = [nc.dram_tensor(n, a.shape, mybir.dt.from_np(a.dtype), kind="ExternalInput").ap() for n, a in ins.items()]
    args.append(nc.dram_tensor("out", (N, D), f32, kind="ExternalOutput").ap())
    gnn_two_layers(nc, *args)
    r = run_bass_kernel_spmd(nc, [ins], core_ids=[0])
    return r.results[0]["out"]
```

```python
import concourse.bass as bass
from concourse import mybir
from contextlib import ExitStack

N = 6250
D = 128
E = 206250
FE = 64
P = 128
NB = (N + P - 1) // P
NBP = NB + 1
NP = NBP * P
PAD_NODE = NB * P
CH = 4
IT = CH * P
IT_BITS = IT.bit_length() - 1
EC = -(-(E + IT) // (P * 16)) * 16
EP = EC * P
SLOTS = 6
DEPTH = 3
K = -(-(E // IT + NB - DEPTH) // SLOTS) * SLOTS + DEPTH
KC = K + 2 * SLOTS
TW = D + 3
SW = D + 2
RW = D + 1
PARTS = 3
LAST = N - (NB - 1) * P
EARLY = 2
NG = 7
NS = NB * 2 // 3 | 1
HG = 3
SKIP = float(1 << 22)
SLOPE = 0.2
EPS = 1e-5
LEAST = -1e30
MOST = 1e38
DST, SRC = 0, 1
assert K >= E // IT + NB and EP - IT >= E and K % SLOTS == DEPTH and KC <= 512 and IT == 1 << IT_BITS

f32, bf16, i32 = mybir.dt.float32, mybir.dt.bfloat16, mybir.dt.int32
ALU, ACT, AX = mybir.AluOpType, mybir.ActivationFunctionType, mybir.AxisListType


class Shared:
    pass




def at_least(eng, s, n):
    if not isinstance(n, int) or n > 0:
        eng.wait_ge(s, n)


def after(i, c, each):
    return i * each + each * (c // SLOTS + 1)


LOOPS = (K - DEPTH) // SLOTS


def rounds(eng, n, first, work):
    with eng.Fori(0, n // 2) as pair:
        i = pair * 2
        for c in range(first, first + 2 * SLOTS):
            work(i, c)
    if n % 2:
        for c in range(first, first + SLOTS):
            work(n - 1, c)


def skewed(eng, step):
    for c in range(DEPTH):
        step(0, c)
    rounds(eng, LOOPS, DEPTH, step)
    for c in range(DEPTH, 2 * DEPTH):
        step(LOOPS, c)


def ahead(eng, work):
    for c in range(SLOTS):
        work(0, c)
    rounds(eng, LOOPS - 1, SLOTS, work)
    for c in range(SLOTS, SLOTS + DEPTH):
        work(LOOPS - 1, c)


def item(i, c):
    return not isinstance(i, int) or 0 <= i * SLOTS + c < K


def setup_stage(nc, g, xn, xt, w, wt, a2, wm, wr, bm, br, src_h, dst_h):
    with ExitStack() as ctx:
        def sb(name, shape, dt=f32):
            return ctx.enter_context(nc.sbuf_tensor(name, shape, dt))

        def sem(name):
            return ctx.enter_context(nc.semaphore(name))

        HW = D + 2
        xts = sb("xt_sb", [P, NBP, P])
        w_sb = sb("w0_sb", [P, D])
        a_sb = sb("a_sb", [P, 2])
        wx = sb("wx", [P, HW])
        ids = sb("ids", [P, 2, EC], i32)
        hii = sb("hii", [P, 2, EC], i32)
        his = sb("his", [P, 2, EC], bf16)
        here = sb("here", [P, 2, EC], bf16)
        er_rest = sb("er_rest", [P, 2, NBP])
        elp = sb("elp", [P, NBP, 2])
        c128 = sb("c128", [P, P])
        cnt = sb("cnt", [P, 2, NBP])
        half = sb("half", [P, NS + 1])
        sign = sb("sign", [P, 2, EC], bf16)
        above = sb("above", [P, NS + 1])
        tot = sb("tot", [P, 2, NBP])
        run = sb("run", [P, 2, NBP])
        toti = sb("toti", [P, 2, NBP], i32)
        nit = sb("nit", [P, 2, NBP])
        itend = sb("itend", [P, 2, NBP])
        dlt = sb("dlt", [P, 2, NBP])
        junk = sb("junk", [P, NBP])
        col = sb("col", [P, 4])
        past = sb("past", [P, 2, KC])
        e0f = sb("e0f", [1, 2, KC])
        has = sb("has", [1, KC])
        low = sb("low", [P, 4])
        padrec = sb("padrec", [P, CH, RW])
        ps = [ctx.enter_context(nc.psum_tensor(f"ps_s{i}", [P, 512], f32)) for i in range(8)]

        s_ld, s_edge, s_tab, s_pad = (sem(f"su_{n}") for n in ("load", "edges", "table_stored", "pad_stored"))
        s_const, s_id, s_wx, s_wxc, s_h, s_hc, s_one, s_fix = (
            sem(f"su_{n}") for n in ("const", "ident", "wx", "wx_copied", "h", "h_copied", "one", "table_made"))
        s_low, s_lowt, s_lowm, s_lowb = (sem(f"su_{n}") for n in ("low", "low_turned", "low_least", "low_spread"))
        s_src, s_sign, s_pass, s_cnt, s_tot, s_col, s_it, s_itc, s_chain, s_padv = (
            sem(f"su_{n}") for n in ("src", "sign", "pass", "counted", "totals", "columns", "items", "items_copied", "chain", "pad_made"))
        block = ctx.enter_context(nc.Block())
        groups = -(-NBP // HG)

        @block.sync
        def _(sp):
            sp.dma_start(ids[:, 0, :], dst_h.rearrange("(p c) -> p c", p=P)).then_inc(s_edge, 16)
            for to, of in ((w_sb[:, :], w), (wx[:, 0:D], wt), (a_sb[:, :], a2),
                           (xts[:, :, :], xt.rearrange("p (b n) -> p b n", n=P)),
                           (g.x[:, :, :], xn.rearrange("(b p) d -> p b d", p=P)),
                           (g.wmr[:, 0:D], wm[0:D, :]), (g.wm2[:, :], wm[D:D + FE, :]), (g.wmr[:, D:2 * D], wr),
                           (g.brow[:, 0, :], bm), (g.brow[:, 1, :], br)):
                sp.dma_start(to, of).then_inc(s_ld, 16)
            sp.dma_start(ids[:, 1, :], src_h.rearrange("(p c) -> p c", p=P)).then_inc(s_edge, 16)
            sp.wait_ge(s_fix, 1)
            sp.dma_start(g.table_d.rearrange("(b p) w -> p b w", p=P), g.table[:, :, :]).then_inc(s_tab, 16)
            sp.wait_ge(s_padv, 2)
            sp.dma_start(g.rec_d[E:E + IT, :].rearrange("(p j) w -> p j w", p=P), padrec[:, :, :]).then_inc(s_pad, 16)
            sp.wait_ge(s_tab, 16)
            sp.wait_ge(s_pad, 16)
            sp.wait_ge(s_ld, 160)

        @block.gpsimd
        def _(pool):
            pool.iota(g.iota[:, :], pattern=[[1, 512]], base=0, channel_multiplier=0, allow_small_or_imprecise_dtypes=True).then_inc(s_const, 1)
            pool.memset(g.ones[:, :], 1.0).then_inc(s_const, 1)
            pool.memset(g.onesb[:, :], 1.0).then_inc(s_const, 1)
            pool.iota(g.part[:, :], pattern=[[0, 1]], base=0, channel_multiplier=1, allow_small_or_imprecise_dtypes=True).then_inc(s_const, 1)
            pool.memset(c128[:, :], float(P)).then_inc(s_const, 1)
            pool.memset(cnt[:, :, NB:NBP], 0.0).then_inc(s_const, 1)
            pool.memset(g.ident[:, :], 0.0).then_inc(s_id, 1)
            pool.memset(g.tri[:, :], 0.0).then_inc(s_id, 1)
            pool.wait_ge(s_id, 2)
            pool.affine_select(out=g.ident[:, :], in_=g.ident[:, :], compare_op=ALU.not_equal, fill=1.0,
                               base=0, pattern=[[-1, P]], channel_multiplier=1).then_inc(s_id, 1)
            pool.affine_select(out=g.tri[:, :], in_=g.tri[:, :], compare_op=ALU.is_ge, fill=1.0,
                               base=0, pattern=[[-1, P]], channel_multiplier=1).then_inc(s_id, 1)
            pool.memset(padrec[:, :, 0:RW - 1], 0.0).then_inc(s_padv, 1)
            pool.memset(padrec[:, :, RW - 1:RW], float(PAD_NODE)).then_inc(s_padv, 1)
            pool.memset(g.acc[:, :, :], 0.0).then_inc(s_const, 1)
            pool.memset(g.erm[:, :, 1:2], LEAST).then_inc(s_const, 1)
            pool.memset(g.erm_parts[:, :, :, 1], 0.0).then_inc(s_const, 1)
            pool.wait_ge(s_id, 3)
            pool.tensor_copy(g.identb[:, :], g.ident[:, :]).then_inc(s_const, 1)
            pool.wait_ge(s_const, 1)
            pool.tensor_copy(g.iotab[:, :], g.iota[:, 0:P]).then_inc(s_const, 1)

        @block.scalar
        def _(act):
            act.wait_ge(s_wx, 1)
            nc.scalar.activation(wx[:, D:HW], ps[7][:, 0:2], ACT.Copy).then_inc(s_wxc, 1)
            for i in range(groups):
                nb = min(HG, NBP - HG * i)
                act.wait_ge(s_h, i + 1)
                nc.scalar.activation(g.table[:, HG * i:HG * i + nb, 0:HW],
                                     ps[i % 4][:, 0:nb * HW].rearrange("p (b w) -> p b w", w=HW), ACT.Copy).then_inc(s_hc, 1)

            def count(n, a):
                nc.scalar.activation(sign[:, a, :], his[:, 1, :], ACT.Sign, bias=half[:, bass.ds(n, 1)],
                                     accum_out=above[:, bass.ds(n, 1)]).then_inc(s_sign, 1)

            act.wait_ge(s_src, 3)
            for a in range(2):
                count(a, a)
            with act.Fori(1, (NS + 1) // 2) as pair:
                for a in range(2):
                    act.wait_ge(s_sign, pair * 2 + a - 1)
                    act.sem_inc(s_pass, 1)
                    count(pair * 2 + a, a)

        @block.tensor
        def _(pe):
            pe.wait_ge(s_ld, 160)
            nc.tensor.matmul(ps[7][:, 0:2], w_sb[:, :], a_sb[:, :], start=True, stop=True).then_inc(s_wx, 1)
            pe.wait_ge(s_wxc, 1)
            for i in range(groups):
                at_least(pe, s_hc, i - 3)
                for n in range(min(HG, NBP - HG * i)):
                    h = nc.tensor.matmul(ps[i % 4][:, n * HW:(n + 1) * HW], xts[:, HG * i + n, :], wx[:, :], start=True, stop=True)
                h.then_inc(s_h, 1)
            pe.wait_ge(s_low, 1)
            pe.wait_ge(s_id, 4)
            pe.wait_ge(s_const, 3)
            nc.tensor.matmul(ps[6][0:1, 0:P], low[:, 0:1], g.ident[:, :], start=True, stop=True).then_inc(s_lowt, 1)
            pe.wait_ge(s_lowm, 1)
            nc.tensor.matmul(ps[6][:, P:P + 1], g.ones[0:1, :], low[0:1, 1:2], start=True, stop=True).then_inc(s_lowb, 1)
            pe.wait_ge(s_cnt, 1)
            nc.tensor.matmul(ps[4][:, 0:2 * NBP], g.ones[:, :], cnt[:, :, :].rearrange("p a b -> p (a b)"), start=True, stop=True).then_inc(s_tot, 1)
            for a in range(2):
                pe.wait_ge(s_col, 1)
                at_least(pe, s_itc, a)
                nc.tensor.matmul(ps[0][:, 0:KC], c128[0:NB, :], past[0:NB, a, :], start=True, stop=True)
                nc.tensor.matmul(ps[1][0:1, 0:KC], col[0:NB, 2 * a + 1:2 * a + 2], past[0:NB, a, :], start=True, stop=True).then_inc(s_it, 1)

        @block.vector
        def _(dve):
            chain = [0]

            def link(ins):
                chain[0] += 1
                ins.then_inc(s_chain, 1)
                dve.wait_ge(s_chain, chain[0])

            dve.wait_ge(s_hc, groups)
            nc.vector.tensor_reduce(low[:, 0:1], g.table[:, :, D], axis=AX.X, op=ALU.min).then_inc(s_low, 1)
            link(nc.vector.tensor_copy(g.erm[:, :, 0], g.table[:, :, D + 1]))
            nc.vector.memset(g.table[:, :, D + 1:SW], 1.0).then_inc(s_one, 1)
            dve.wait_ge(s_lowt, 1)
            nc.vector.tensor_reduce(low[0:1, 1:2], ps[6][0:1, 0:P], axis=AX.X, op=ALU.min).then_inc(s_lowm, 1)
            dve.wait_ge(s_edge, 16)
            link(nc.vector.tensor_scalar(hii[:, 0, :], ids[:, 0, :], 7, None, ALU.arith_shift_right))
            link(nc.vector.tensor_copy(his[:, 0, :], hii[:, 0, :]))
            dve.wait_ge(s_lowb, 1)
            link(nc.vector.tensor_copy(g.elmin[:, :], ps[6][:, P:P + 1]))
            link(nc.vector.tensor_scalar(g.ermin[:, :, :], g.erm[:, :, 0:1], g.elmin[:, 0:1], None, ALU.add))
            for h in range(PARTS):
                link(nc.vector.tensor_copy(g.erm_parts[:, :, h, 0], (g.erm[:, :, 0], er_rest[:, 0, :], er_rest[:, 1, :])[h]))
                if h + 1 < PARTS:
                    link(nc.vector.tensor_tensor(er_rest[:, h, :], (g.erm[:, :, 0], er_rest[:, 0, :])[h], g.erm_parts[:, :, h, 0], ALU.subtract))
            link(nc.vector.tensor_scalar(elp[:, :, 0], g.table[:, :, D], g.elmin[:, 0:1], None, ALU.subtract))
            parts = g.table[:, :, SW:TW].bitcast(bf16)
            link(nc.vector.tensor_copy(parts[:, :, 0], elp[:, :, 0]))
            link(nc.vector.tensor_tensor(elp[:, :, 1], elp[:, :, 0], parts[:, :, 0], ALU.subtract))
            dve.wait_ge(s_one, 1)
            nc.vector.tensor_copy(parts[:, :, 1], elp[:, :, 1]).then_inc(s_fix, 1)
            dve.wait_ge(s_edge, 32)
            nc.vector.tensor_scalar(hii[:, 1, :], ids[:, 1, :], 7, None, ALU.arith_shift_right).then_inc(s_src, 1)
            dve.wait_ge(s_src, 1)
            nc.vector.tensor_copy(his[:, 1, :], hii[:, 1, :]).then_inc(s_src, 1)
            dve.wait_ge(s_const, 11)
            nc.vector.tensor_scalar(half[:, :], g.iota[:, 0:NS + 1], -1.0, 0.5, ALU.mult, ALU.add).then_inc(s_src, 1)
            dve.wait_ge(s_src, 3)

            def count(slot, a, b):
                nc.vector.tensor_scalar(here[:, slot, :], his[:, a, :], g.iota[:, bass.ds(b, 1)], 0.0, ALU.is_equal, ALU.add,
                                        accum_out=cnt[:, a, bass.ds(b, 1)]).then_inc(s_chain, 1)

            with dve.Fori(0, NB - NS) as b:
                for a in range(2):
                    dve.wait_ge(s_chain, b * 2 + chain[0] + a - 1)
                    count(a, a, b + a * NS)
            chain[0] += 2 * (NB - NS)
            dve.wait_ge(s_chain, chain[0] - 1)
            count(0, DST, NB - NS)
            with dve.Fori(0, NS // 2) as pair:
                for slot in (1, 0):
                    dve.wait_ge(s_chain, pair * 2 + chain[0] + 1 - slot)
                    count(slot, DST, pair * 2 + NB - NS + 2 - slot)
            chain[0] += NS
            dve.wait_ge(s_chain, chain[0])
            dve.wait_ge(s_sign, NS + 1)
            link(nc.vector.tensor_tensor(cnt[:, SRC, 0:NS], above[:, 0:NS], above[:, 1:NS + 1], ALU.subtract))
            link(nc.vector.tensor_scalar(cnt[:, SRC, 0:NS], cnt[:, SRC, 0:NS], 0.5, None, ALU.mult))
            nc.vector.tensor_copy(low[:, 2:3], cnt[:, 0, 0:1]).then_inc(s_cnt, 1)
            dve.wait_ge(s_tot, 1)
            link(nc.vector.tensor_copy(tot[:, :, :].rearrange("p a b -> p (a b)"), ps[4][:, 0:2 * NBP]))
            link(nc.vector.tensor_scalar(toti[:, :, :], tot[:, :, :], float(IT - 1), None, ALU.add))
            link(nc.vector.tensor_scalar(toti[:, :, :], toti[:, :, :], IT_BITS, None, ALU.arith_shift_right))
            link(nc.vector.tensor_copy(nit[:, :, :], toti[:, :, :]))
            for a in range(2):
                link(nc.vector.tensor_tensor_scan(itend[:, a, :], g.ones[:, 0:NBP], nit[:, a, :], 0.0, ALU.mult, ALU.add))
            link(nc.vector.tensor_tensor_scan(run[:, SRC, :], g.ones[:, 0:NBP], tot[:, SRC, :], 0.0, ALU.mult, ALU.add))
            link(nc.vector.tensor_tensor(g.base[:, :], run[:, SRC, :], tot[:, SRC, :], ALU.subtract))
            link(nc.vector.scalar_tensor_tensor(dlt[:, :, :], nit[:, :, :], -float(IT), tot[:, :, :], ALU.mult, ALU.add))
            for a in range(2):
                for i, t in enumerate((itend, dlt)):
                    link(nc.vector.scalar_tensor_tensor(junk[:, :], t[:, a, :], 1.0, g.ident[:, 0:NBP], ALU.mult, ALU.mult,
                                                        accum_out=col[:, 2 * a + i:2 * a + i + 1]))
                link(nc.vector.tensor_scalar(past[:, a, :], g.iota[:, 0:KC], col[:, 2 * a:2 * a + 1], None, ALU.is_ge))
            nc.vector.tensor_copy(low[:, 3:4], col[:, 0:1]).then_inc(s_col, 1)
            for a, cap in ((DST, EP - IT), (SRC, E)):
                dve.wait_ge(s_it, a + 1)
                link(nc.vector.tensor_copy(g.b128[:, a, :], ps[0][:, 0:KC]))
                if a == DST:
                    link(nc.vector.tensor_scalar(g.nid[:, :], g.b128[:, DST, :], g.part[:, 0:1], None, ALU.add))
                link(nc.vector.tensor_scalar(g.bt[:, a, :], g.b128[0:1, a, :], 1.0 / P, None, ALU.mult))
                link(nc.vector.scalar_tensor_tensor(e0f[:, a, :], g.iota[0:1, 0:KC], float(IT), ps[1][0:1, 0:KC], ALU.mult, ALU.add))
                nc.vector.tensor_scalar(g.e0t[:, a, :], e0f[:, a, :], float(cap), None, ALU.min).then_inc(s_itc, 1)
                if a == DST:
                    link(nc.vector.tensor_scalar(e0f[:, a, :], e0f[:, a, :], float(E), None, ALU.min))
                    link(nc.vector.memset(has[:, :], 0.0))
                    link(nc.vector.tensor_tensor(has[:, 0:KC - 1], e0f[:, a, 1:KC], e0f[:, a, 0:KC - 1], ALU.subtract))
                    link(nc.vector.tensor_scalar(g.filled[:, :], has[:, :], float(P - 1), None, ALU.add))
                    link(nc.vector.tensor_scalar(g.filled[:, :], g.filled[:, :], P.bit_length() - 1, None, ALU.arith_shift_right))
                    link(nc.vector.tensor_scalar(g.filled[:, :], g.filled[:, :], 1, None, ALU.max))
                    link(nc.vector.tensor_scalar(has[:, :], g.filled[:, :], 16.0, None, ALU.mult))
                    for s in range(SLOTS):
                        link(nc.vector.tensor_tensor_scan(e0f[:, a, s:KC:SLOTS], g.ones[0:1, 0:len(range(s, KC, SLOTS))], has[:, s:KC:SLOTS],
                                                          0.0, ALU.mult, ALU.add))
                    link(nc.vector.tensor_copy(g.moved[:, :], e0f[:, a, :]))


def first_layer_stage(nc, g, meta_h):
    with ExitStack() as ctx:
        def sb(name, shape, dt=f32):
            return ctx.enter_context(nc.sbuf_tensor(name, shape, dt))

        def sem(name):
            return ctx.enter_context(nc.semaphore(name))

        def bank(name, dt=f32):
            return ctx.enter_context(nc.psum_tensor(name, [P, CH * P], dt))

        meta = sb("meta1", [P, SLOTS, CH, 2], i32)
        rows = sb("rows", [P, SLOTS, CH, TW])
        rel = sb("rel1", [P, 2, CH])
        hot = sb("hot1", [P, DEPTH, CH, P], bf16)
        apart = sb("apart", [P, CH, P], bf16)
        hot_t = sb("hot_t1", [P, 2, CH * P], bf16)
        seen = sb("seen", [P, 2, CH * P], bf16)
        wgt = sb("wgt", [P, 2, CH, P])
        mx = sb("mx", [P, 2, 5])
        sc = sb("sc", [P, 2, 4, CH])
        fade = sb("fade", [P, DEPTH, 1])
        ps_t = [bank(f"ps_t{i}", bf16) for i in range(2)]
        ps_x = [bank(f"ps_x{i}") for i in range(2)]
        ps_o = [bank(f"ps_o{i}") for i in range(2)]
        ps_e = [bank(f"ps_e{i}") for i in range(2)]

        meta_in = [sem(f"meta_in{i}") for i in range(SLOTS)]
        gathered = [sem(f"gathered{i}") for i in range(SLOTS)]
        (s_rel, s_hot, s_turned, s_hot_t, s_spread, s_max, s_sum, s_leaky, s_m, s_grown, s_kept, s_picked, s_z, s_lz,
         s_q, s_p, s_wgt, s_out, s_fade, s_acc, s_pass, s_apart, s_m1, s_m2, s_blank) = (
            sem(f"l1_{n}") for n in ("rel", "hot", "turned", "hot_t", "spread", "max", "sum", "leaky", "m",
                                     "grown", "kept", "picked", "z", "lz", "q", "p", "wgt", "out", "fade", "acc", "pass",
                                     "apart", "m1", "m2", "blank"))
        block = ctx.enter_context(nc.Block())

        @block.sync
        def _(sp):
            def load(i, c):
                s, k = c % SLOTS, i * SLOTS + c
                e0 = sp.value_load(g.e0t[0:1, DST, bass.ds(k, 1)], min_val=0, max_val=EP - IT)
                at_least(sp, s_rel, k - SLOTS + 1)
                at_least(sp, s_out, k - SLOTS + 1)
                sp.dma_start(meta[:, s, :, :], meta_h[bass.ds(e0, IT), :].rearrange("(j p) w -> p j w", p=P)).then_inc(meta_in[s], 16)

            ahead(sp, load)
            load(LOOPS - 1, SLOTS + DEPTH)
            sp.wait_ge(meta_in[K % SLOTS], after(LOOPS - 1, SLOTS + DEPTH, 16))

        @block.gpsimd
        def _(pool):
            def gather(i, c):
                s, k = c % SLOTS, i * SLOTS + c
                filled = pool.value_load(g.filled[0:1, bass.ds(k, 1)], min_val=0, max_val=CH)
                pool.wait_ge(meta_in[s], after(i, c, 16))
                at_least(pool, s_out, k - SLOTS + 1)
                pool.sem_inc(s_pass, 1)
                for j in range(CH):
                    with pool.If(filled > j):
                        pool.indirect_dma_start(out=rows[:, s, j, :], out_offset=None, in_=g.table_d,
                                                in_offset=bass.IndirectOffsetOnAxis(ap=meta[:, s, j, 0:1], axis=0)).then_inc(gathered[s], 16)

            nc.gpsimd.memset(rows[:, :, :, :], 0.0).then_inc(s_blank, 1)
            pool.wait_ge(s_blank, 1)
            ahead(pool, gather)

        @block.scalar
        def _(act):
            def mark(i, c):
                k = i * SLOTS + c
                act.wait_ge(s_rel, k + 1)
                at_least(act, s_hot, k)
                for j in range(CH):
                    apart_j = nc.scalar.activation(apart[:, j, :], g.iotab[:, :], ACT.Abs, bias=rel[:, c % 2, j:j + 1])
                apart_j.then_inc(s_apart, 1)
                act.wait_ge(s_apart, k + 1)
                at_least(act, s_wgt, k - 2)
                at_least(act, s_turned, k - 2)
                nc.scalar.activation(hot[:, c % DEPTH, :, :], apart[:, :, :], ACT.Relu, scale=-1.0, bias=1.0).then_inc(s_hot, 1)

            def step(i, c):
                k = i * SLOTS + c
                if isinstance(k, int) and k == 0:
                    mark(i, c)
                if item(i, c - 2):
                    act.wait_ge(s_q, k - 1)
                    at_least(act, s_wgt, k - 3)
                    nc.scalar.activation(sc[:, c % 2, 3, :], sc[:, c % 2, 2, :], ACT.Exp).then_inc(s_p, 1)
                if item(i, c):
                    act.wait_ge(s_turned, k + 1)
                    at_least(act, s_picked, k - 1)
                    at_least(act, s_max, k - 1)
                    nc.scalar.activation(hot_t[:, c % 2, :], ps_t[c % 2][:, :], ACT.Copy).then_inc(s_hot_t, 1)
                if item(i, c - 1):
                    act.wait_ge(s_grown, k)
                    at_least(act, s_acc, k - 3)
                    nc.scalar.activation(fade[:, (c - 1) % DEPTH, :], mx[:, (c - 1) % 2, 4:5], ACT.Exp, scale=-1.0).then_inc(s_fade, 1)
                if item(i, c + 1):
                    mark(i, c + 1)

            skewed(act, step)

        @block.tensor
        def _(pe):
            def step(i, c):
                k = i * SLOTS + c
                u, v = c % 2, (c - 1) % 2
                b = pe.value_load(g.bt[0:1, DST, bass.ds(k - 1, 1)], min_val=0, max_val=NB) if item(i, c - 1) else None
                if item(i, c):
                    pe.wait_ge(s_hot, k + 1)
                    at_least(pe, s_hot_t, k - 1)
                    for j in range(CH):
                        mm = nc.tensor.transpose(ps_t[u][:, j * P:(j + 1) * P], hot[:, c % DEPTH, j, :], g.identb[:, :])
                    mm.then_inc(s_turned, 1)
                if item(i, c):
                    pe.wait_ge(gathered[c % SLOTS], pe.value_load(g.moved[0:1, bass.ds(k, 1)], min_val=16, max_val=16 * CH * KC))
                    at_least(pe, s_max, k - 1)
                    for j in range(CH):
                        parts = rows[:, c % SLOTS, j, SW:TW].bitcast(bf16)
                        for h in range(2):
                            mm = nc.tensor.matmul(ps_x[u][:, j * P:(j + 1) * P], parts[:, h:h + 1].to_broadcast([P, P]), g.identb[:, :],
                                                  start=h == 0, stop=h == 1)
                    mm.then_inc(s_spread, 1)
                if b is not None:
                    pe.wait_ge(s_m2, k)
                    pe.wait_ge(s_hot_t, k)
                    at_least(pe, s_q, k - 2)
                    for j in range(CH):
                        for h in range(PARTS):
                            mm = nc.tensor.matmul(ps_e[v][:, 2 * j:2 * j + 2], hot_t[:, v, j * P:(j + 1) * P], g.erm_parts[:, bass.ds(b, 1), h, :],
                                                  start=h == 0, stop=h == PARTS - 1)
                    mm.then_inc(s_picked, 1)
                if item(i, c - 2):
                    pe.wait_ge(s_wgt, k - 1)
                    at_least(pe, s_acc, k - 3)
                    for j in range(CH):
                        mm = nc.tensor.matmul(ps_o[u][:, 0:SW], wgt[:, u, j, :], rows[:, (c - 2) % SLOTS, j, 0:SW], start=j == 0, stop=j == CH - 1)
                    mm.then_inc(s_out, 1)

            skewed(pe, step)

        @block.vector
        def _(dve):
            loaded = {}

            def block_of(i, c):
                if not item(i, c):
                    return None
                if (id(i), c) not in loaded:
                    loaded[id(i), c] = load_block(i, c)
                return loaded[id(i), c]

            def load_block(i, c):
                return bass.ds(dve.value_load(g.bt[0:1, DST, bass.ds(i * SLOTS + c, 1)], min_val=0, max_val=NB), 1)

            def within(i, c):
                k = i * SLOTS + c
                dve.wait_ge(meta_in[c % SLOTS], after(i, c, 16))
                nc.vector.tensor_scalar(rel[:, c % 2, :], meta[:, c % SLOTS, :, 1], -1.0, g.b128[:, DST, bass.ds(k, 1)], ALU.mult, ALU.add).then_inc(s_rel, 1)

            def step(i, c):
                k = i * SLOTS + c
                u, v = c % 2, (c - 1) % 2
                s2 = (c - 2) % SLOTS
                b1 = block_of(i, c - 1)
                one, two = item(i, c - 1), item(i, c - 2)
                er_m = ps_e[u][:, 0:2 * CH].rearrange("p (j w) -> p j w", w=2)
                if isinstance(k, int) and k == 0:
                    within(i, c)
                if one:
                    dve.wait_ge(s_spread, k)
                    dve.wait_ge(s_hot_t, k)
                    dve.sem_inc(s_pass, 1)
                    nc.vector.tensor_tensor_reduce(seen[:, v, :], ps_x[v][:, :], hot_t[:, v, :], 1.0, 0.0, ALU.mult, ALU.max,
                                                   mx[:, v, 0:1]).then_inc(s_max, 1)
                b3 = block_of(i, c - 3)
                if two:
                    dve.wait_ge(s_picked, k - 1)
                    nc.vector.tensor_tensor(sc[:, u, 0, :], rows[:, s2, :, D], er_m[:, :, 0], ALU.add).then_inc(s_z, 1)
                if one:
                    dve.wait_ge(s_max, k)
                    nc.vector.tensor_tensor(mx[:, v, 1:2], mx[:, v, 0:1], g.ermin[:, b1, 0], ALU.add).then_inc(s_sum, 1)
                if two:
                    dve.wait_ge(s_z, k - 1)
                    nc.vector.scalar_tensor_tensor(sc[:, u, 1, :], sc[:, u, 0, :], SLOPE, sc[:, u, 0, :], ALU.mult, ALU.max).then_inc(s_lz, 1)
                if one:
                    dve.wait_ge(s_sum, k)
                    nc.vector.scalar_tensor_tensor(mx[:, v, 2:3], mx[:, v, 1:2], SLOPE, mx[:, v, 1:2], ALU.mult, ALU.max).then_inc(s_leaky, 1)
                if two:
                    dve.wait_ge(s_lz, k - 1)
                    nc.vector.tensor_tensor(sc[:, u, 2, :], sc[:, u, 1, :], er_m[:, :, 1], ALU.subtract).then_inc(s_q, 1)
                if one:
                    dve.wait_ge(s_leaky, k)
                    at_least(dve, s_kept, k - 1)
                    nc.vector.tensor_tensor(mx[:, v, 3:4], mx[:, v, 2:3], g.erm[:, b1, 1], ALU.max).then_inc(s_m, 1)
                if one:
                    dve.wait_ge(s_m, k)
                    m_parts = g.erm_parts[:, b1, :, 1]
                    nc.vector.tensor_scalar(m_parts[:, :, 0], mx[:, v, 3:4], 0.0, None, ALU.add).then_inc(s_m1, 1)
                if item(i, c + 1):
                    within(i, c + 1)
                if one:
                    dve.wait_ge(s_m1, k)
                    nc.vector.tensor_tensor(m_parts[:, :, 1], mx[:, v, 3:4], m_parts[:, :, 0], ALU.subtract).then_inc(s_m2, 1)
                if b3 is not None:
                    dve.wait_ge(s_out, k - 2)
                    dve.wait_ge(s_fade, k - 2)
                    at_least(dve, s_acc, k - 3)
                    nc.vector.scalar_tensor_tensor(g.acc[:, b3, :], g.acc[:, b3, :], fade[:, c % DEPTH, :],
                                                   ps_o[v][:, 0:SW].unsqueeze(1), ALU.mult, ALU.add).then_inc(s_acc, 1)
                if one:
                    dve.wait_ge(s_m2, k)
                    nc.vector.scalar_tensor_tensor(mx[:, v, 4:5], m_parts[:, :, 0], g.erm[:, b1, 1], m_parts[:, :, 1],
                                                   ALU.subtract, ALU.add).then_inc(s_grown, 1)
                    dve.wait_ge(s_grown, k)
                    nc.vector.tensor_tensor(g.erm[:, b1, 1], m_parts[:, :, 0], m_parts[:, :, 1], ALU.add).then_inc(s_kept, 1)
                if two:
                    dve.wait_ge(s_p, k - 1)
                    nc.vector.scalar_tensor_tensor(wgt[:, u, :, :], sc[:, u, 3, :].unsqueeze(2).to_broadcast([P, CH, P]), MOST,
                                                   hot[:, (c - 2) % DEPTH, :, :], ALU.min, ALU.mult).then_inc(s_wgt, 1)

            skewed(dve, step)


def norm_project_stage(nc, g):
    with ExitStack() as ctx:
        def sb(name, shape, dt=f32):
            return ctx.enter_context(nc.sbuf_tensor(name, shape, dt))

        def sem(name):
            return ctx.enter_context(nc.semaphore(name))

        den = sb("den", [P, 2, NB])
        st = sb("n1_st", [P, 6, NB])
        square = sb("n1_square", [P, NG, D])
        turned = sb("turned", [P, 2, NG, P])
        rest = sb("rest", [P, NG, D])
        bias = sb("bias", [P, D])
        ps_t = ctx.enter_context(nc.psum_tensor("ps_f", [P, 1024], f32))
        ps_y = [ctx.enter_context(nc.psum_tensor(f"ps_y{i}", [P, 1024], f32)) for i in range(2)]
        ps_r = ctx.enter_context(nc.psum_tensor("ps_r", [P, 1024], f32))
        (s_half, s_row, s_wide, s_bias, s_den, s_inv, s_new, s_mean, s_sq, s_var, s_root, s_rstd, s_norm, s_turned, s_cp,
         s_y, s_a, s_r, s_b, s_c, s_base, s_sum) = (
            sem(f"np_{n}") for n in ("halved", "bias_row", "bias_wide", "bias", "denominator", "inverse", "new", "mean",
                                     "squares", "variance", "root", "rstd", "normed", "turned", "copied", "y", "part_a",
                                     "rest", "part_b", "part_c", "base", "sum"))
        block = ctx.enter_context(nc.Block())
        groups = [range(b, min(b + NG, NB)) for b in range(0, NB, NG)]

        def group(q):
            return groups[q] if 0 <= q < len(groups) else None

        def of(tensor, bs):
            return tensor[:, bs[0]:bs[-1] + 1, :]

        def bank(ps, bs):
            return ps[:, 0:len(bs) * P].rearrange("p (b n) -> p b n", n=P)

        @block.gpsimd
        def _(pool):
            pool.wait_ge(s_bias, 1)
            for q, bs in enumerate(groups):
                pool.wait_ge(s_norm, q + 1)
                nc.gpsimd.tensor_tensor(of(g.sums, bs), of(g.x, bs), bias[:, :].unsqueeze(1).to_broadcast([P, len(bs), D]), ALU.add).then_inc(s_base, 1)

        @block.scalar
        def _(act):
            nc.scalar.activation(g.wmr[:, 0:D], g.wmr[:, 0:D], ACT.Copy, scale=0.5).then_inc(s_half, 1)
            nc.scalar.activation(g.wm2[:, :], g.wm2[:, :], ACT.Copy, scale=0.5).then_inc(s_half, 1)
            act.wait_ge(s_wide, 1)
            nc.scalar.activation(bias[:, :], ps_r[:, 0:D], ACT.Copy).then_inc(s_bias, 1)
            for q in range(len(groups) + 2):
                new, mid, old = group(q), group(q - 1), group(q - 2)
                if mid:
                    act.wait_ge(s_var, q)
                    nc.scalar.activation(st[:, 4, mid[0]:mid[-1] + 1], st[:, 3, mid[0]:mid[-1] + 1], ACT.Sqrt).then_inc(s_root, 1)
                if old:
                    act.wait_ge(s_y, q - 1)
                    nc.scalar.activation(of(g.parts[:, :, 0, :], old), bank(ps_y[q % 2], old), ACT.Copy).then_inc(s_a, 1)
                if new:
                    act.wait_ge(s_mean, q + 1)
                    at_least(act, s_sq, q)
                    for n, b in enumerate(new):
                        sq = nc.scalar.activation(square[:, n, :], g.x[:, b, :], ACT.Square, bias=st[:, 1, b:b + 1], accum_out=st[:, 2, b:b + 1])
                    sq.then_inc(s_sq, 1)
                if mid:
                    act.wait_ge(s_turned, q)
                    at_least(act, s_y, q - 2)
                    nc.scalar.activation(turned[:, (q - 1) % 2, 0:len(mid), :], bank(ps_t, mid), ACT.Copy).then_inc(s_cp, 1)
                if old:
                    act.wait_ge(s_r, q - 1)
                    nc.scalar.activation(of(g.parts[:, :, 1, :], old), rest[:, 0:len(old), :], ACT.Copy).then_inc(s_b, 1)

        @block.tensor
        def _(pe):
            pe.wait_ge(s_row, 1)
            nc.tensor.matmul(ps_r[:, 0:D], g.ones[0:1, :], g.brow[:, 2, :], start=True, stop=True).then_inc(s_wide, 1)
            pe.wait_ge(s_half, 2)
            pe.wait_ge(s_bias, 1)
            for q, bs in enumerate(groups):
                pe.wait_ge(s_norm, q + 1)
                at_least(pe, s_cp, q)
                for n, b in enumerate(bs):
                    mm = nc.tensor.transpose(ps_t[:, n * P:(n + 1) * P], g.x[:, b, :], g.ident[:, :])
                mm.then_inc(s_turned, 1)
                pe.wait_ge(s_cp, q + 1)
                at_least(pe, s_r, q - 1)
                for n in range(len(bs)):
                    nc.tensor.matmul(ps_y[q % 2][:, n * D:(n + 1) * D], turned[:, q % 2, n, :], g.wmr[:, 0:D], start=True, stop=True)
                at_least(pe, s_sum, q)
                for n in range(len(bs)):
                    mm = nc.tensor.matmul(ps_r[:, n * D:(n + 1) * D], turned[:, q % 2, n, :], g.wmr[:, D:2 * D], start=True, stop=True)
                mm.then_inc(s_y, 1)

        @block.vector
        def _(dve):
            nc.vector.scalar_tensor_tensor(g.brow[:, 2, :], g.brow[:, 0, :], 0.5, g.brow[:, 1, :], ALU.mult, ALU.add).then_inc(s_row, 1)
            nc.vector.tensor_scalar(den[:, 0, :], g.acc[:, 0:NB, SW - 1], 1e-38, None, ALU.max).then_inc(s_den, 1)
            dve.wait_ge(s_den, 1)
            nc.vector.reciprocal(den[:, 1, :], den[:, 0, :]).then_inc(s_inv, 1)
            dve.wait_ge(s_inv, 1)
            for q in range(len(groups) + 2):
                new, mid, old = group(q), group(q - 1), group(q - 2)
                if new:
                    for b in new:
                        row = nc.vector.scalar_tensor_tensor(g.x[:, b, :], g.acc[:, b, 0:D], den[:, 1, b:b + 1], g.x[:, b, :], ALU.mult, ALU.add,
                                                             accum_out=st[:, 0, b:b + 1])
                    row.then_inc(s_new, 1)
                    dve.wait_ge(s_new, q + 1)
                    nc.vector.tensor_scalar(st[:, 1, new[0]:new[-1] + 1], st[:, 0, new[0]:new[-1] + 1], -1.0 / D, None, ALU.mult).then_inc(s_mean, 1)
                if mid:
                    dve.wait_ge(s_sq, q)
                    nc.vector.tensor_scalar(st[:, 3, mid[0]:mid[-1] + 1], st[:, 2, mid[0]:mid[-1] + 1], 1.0 / D, EPS, ALU.mult, ALU.add).then_inc(s_var, 1)
                if mid:
                    dve.wait_ge(s_root, q)
                    nc.vector.reciprocal(st[:, 5, mid[0]:mid[-1] + 1], st[:, 4, mid[0]:mid[-1] + 1]).then_inc(s_rstd, 1)
                    dve.wait_ge(s_rstd, q)
                    dve.wait_ge(s_mean, q)
                    for b in mid:
                        row = nc.vector.tensor_scalar(g.x[:, b, :], g.x[:, b, :], st[:, 1, b:b + 1], st[:, 5, b:b + 1], ALU.add, ALU.mult)
                    row.then_inc(s_norm, 1)
                if old:
                    dve.wait_ge(s_a, q - 1)
                    at_least(dve, s_c, q - 2)
                    nc.vector.tensor_tensor(rest[:, 0:len(old), :], bank(ps_y[q % 2], old), of(g.parts[:, :, 0, :], old), ALU.subtract).then_inc(s_r, 1)
                    dve.wait_ge(s_base, q - 1)
                    nc.vector.tensor_tensor(of(g.sums, old), of(g.sums, old), bank(ps_r, old), ALU.add).then_inc(s_sum, 1)
                    dve.wait_ge(s_b, q - 1)
                    nc.vector.tensor_tensor(of(g.parts[:, :, 2, :], old), rest[:, 0:len(old), :], of(g.parts[:, :, 1, :], old), ALU.subtract).then_inc(s_c, 1)
            nc.vector.memset(g.parts[:, NB, :, :], 0.0)
            nc.vector.memset(g.sums[:, NB, :], 0.0)


def record_stage(nc, g, meta_h, dst_h, feat_h):
    with ExitStack() as ctx:
        def sb(name, shape, dt=f32):
            return ctx.enter_context(nc.sbuf_tensor(name, shape, dt))

        def sem(name):
            return ctx.enter_context(nc.semaphore(name))

        meta = sb("meta2", [P, SLOTS, CH, 2], i32)
        dsts = sb("dsts", [P, SLOTS, IT], i32)
        feat = sb("feat", [FE, SLOTS, IT])
        rec = sb("rec2", [P, SLOTS, CH, RW])
        rel = sb("rel2", [P, 2, CH])
        far = sb("far", [P, 2, 2, CH])
        shifted = sb("shifted", [P, 2, CH], i32)
        blk = sb("blk", [P, 2, CH])
        of = sb("of", [P, 2, CH, NBP], bf16)
        place = sb("place", [P, 2, CH, NBP])
        mine = sb("mine", [P, 2, CH, NBP])
        pos = sb("pos", [P, 2, CH])
        apart = sb("apart2", [P, IT], bf16)
        hot_t = sb("hot_t2", [P, 2, IT], bf16)
        to = sb("to", [P, SLOTS, CH], i32)
        ps_p = [ctx.enter_context(nc.psum_tensor(f"ps_p{i}", [P, 512], f32)) for i in range(2)]
        ps_g = [ctx.enter_context(nc.psum_tensor(f"ps_g{i}", [P, 512], f32)) for i in range(2)]
        edge_in = [sem(f"edge_in{i}") for i in range(SLOTS)]
        scattered = [sem(f"scattered{i}") for i in range(SLOTS)]
        (s_rel, s_src, s_far, s_out_of, s_shift, s_blk, s_of, s_ranked, s_place, s_base, s_mine, s_pos, s_to,
         s_apart, s_hot_t, s_got, s_rec, s_pass) = (
            sem(f"rc_{n}") for n in ("rel", "src", "far", "outside", "shifted", "blk", "of", "ranked", "place", "base", "mine",
                                     "pos", "to", "apart", "hot_t", "got", "rec", "pass"))
        block = ctx.enter_context(nc.Block())

        @block.sync
        def _(sp):
            def load(i, c):
                s, k = c % SLOTS, i * SLOTS + c
                again = not isinstance(i, int) or c >= SLOTS
                moved = sp.value_load(g.moved[0:1, bass.ds(k - SLOTS, 1)], min_val=16, max_val=16 * CH * KC) if again else None
                e0 = sp.value_load(g.e0t[0:1, DST, bass.ds(k, 1)], min_val=0, max_val=EP - IT)
                if again:
                    sp.wait_ge(scattered[s], moved)
                sp.dma_start(meta[:, s, :, :], meta_h[bass.ds(e0, IT), :].rearrange("(j p) w -> p j w", p=P)).then_inc(edge_in[s], 16)
                sp.dma_start(dsts[:, s, :], dst_h[bass.ds(e0, IT)].unsqueeze(0).to_broadcast([P, IT])).then_inc(edge_in[s], 16)
                sp.dma_start(feat[:, s, :], feat_h[:, bass.ds(e0, IT)]).then_inc(edge_in[s], 16)

            ahead(sp, load)
            last = [(k % SLOTS, sp.value_load(g.moved[0:1, k:k + 1], min_val=16, max_val=16 * CH * KC)) for k in range(K - SLOTS, K)]
            for s, moved in last:
                sp.wait_ge(scattered[s], moved)
                sp.sem_inc(s_pass, 1)

        @block.gpsimd
        def _(pool):
            def scatter(i, c):
                s, k = c % SLOTS, i * SLOTS + c
                filled = pool.value_load(g.filled[0:1, bass.ds(k, 1)], min_val=0, max_val=CH)
                pool.wait_ge(s_to, k + 1)
                pool.wait_ge(s_src, k + 1)
                pool.wait_ge(s_rec, k + 1)
                pool.sem_inc(s_pass, 1)
                for j in range(CH):
                    with pool.If(filled > j):
                        pool.indirect_dma_start(out=g.rec_d, out_offset=bass.IndirectOffsetOnAxis(ap=to[:, s, j:j + 1], axis=0),
                                                in_=rec[:, s, j, :], in_offset=None,
                                                bounds_check=E - 1, oob_is_err=False).then_inc(scattered[s], 16)

            ahead(pool, scatter)

        @block.scalar
        def _(act):
            def step(i, c):
                k = i * SLOTS + c
                if item(i, c):
                    act.wait_ge(edge_in[c % SLOTS], after(i, c, 48))
                    at_least(act, s_hot_t, k)
                    act.sem_inc(s_pass, 1)
                    nc.scalar.activation(apart[:, :], dsts[:, c % SLOTS, :], ACT.Abs, bias=g.nid[:, bass.ds(k, 1)], scale=-1.0).then_inc(s_apart, 1)
                    act.wait_ge(s_apart, k + 1)
                    at_least(act, s_got, k - 1)
                    nc.scalar.activation(hot_t[:, c % 2, :], apart[:, :], ACT.Relu, scale=-1.0, bias=1.0).then_inc(s_hot_t, 1)
                if item(i, c - 1):
                    act.wait_ge(s_got, k)
                    act.wait_ge(edge_in[(c - 1) % SLOTS], after(i, c - 1, 48))
                    nc.scalar.activation(rec[:, (c - 1) % SLOTS, :, 0:D], ps_g[(c - 1) % 2][:, :].rearrange("p (j n) -> p j n", n=P),
                                         ACT.Copy).then_inc(s_rec, 1)

            skewed(act, step)

        @block.tensor
        def _(pe):
            def step(i, c):
                k = i * SLOTS + c
                if not item(i, c):
                    return
                u, s = c % 2, c % SLOTS
                b = pe.value_load(g.bt[0:1, DST, bass.ds(k, 1)], min_val=0, max_val=NB)
                pe.wait_ge(s_of, k + 1)
                at_least(pe, s_place, k - 1)
                at_least(pe, s_base, k - 1)
                nc.tensor.matmul(ps_p[u][:, 0:CH * NBP], g.tri[:, :], of[:, u, :, :].rearrange("p j b -> p (j b)"), start=True, stop=False)
                for j in range(CH - 1):
                    nc.tensor.matmul(ps_p[u][:, (j + 1) * NBP:CH * NBP].rearrange("p (j b) -> p j b", b=NBP), g.onesb[:, :],
                                     of[:, u, j, :].unsqueeze(1).to_broadcast([P, CH - 1 - j, NBP]), start=False, stop=j == CH - 2)
                for j in range(CH):
                    mm = nc.tensor.matmul(ps_p[u][:, CH * NBP:(CH + 1) * NBP], g.onesb[:, :], of[:, u, j, :], start=j == 0, stop=j == CH - 1)
                mm.then_inc(s_ranked, 1)
                pe.wait_ge(s_hot_t, k + 1)
                at_least(pe, s_rec, k - 1)
                for j in range(CH):
                    to_j = ps_g[u][:, j * P:(j + 1) * P]
                    for h in range(PARTS):
                        nc.tensor.matmul(to_j, hot_t[:, u, j * P:(j + 1) * P], g.parts[:, bass.ds(b, 1), h, :], start=h == 0, stop=False)
                    mm = nc.tensor.matmul(to_j, feat[:, s, j * P:(j + 1) * P], g.wm2[:, :], start=False, stop=True)
                mm.then_inc(s_got, 1)

            skewed(pe, step)

        @block.vector
        def _(dve):
            def step(i, c):
                k = i * SLOTS + c
                u, v, s = c % 2, (c - 1) % 2, c % SLOTS
                new, old = item(i, c), item(i, c - 1)
                if new:
                    dve.wait_ge(edge_in[s], after(i, c, 48))
                    at_least(dve, s_far, k - 1)
                    nc.vector.tensor_scalar(rel[:, u, :], meta[:, s, :, 1], g.b128[:, DST, bass.ds(k, 1)], None, ALU.subtract).then_inc(s_rel, 1)
                    at_least(dve, s_blk, k - 1)
                    nc.vector.tensor_scalar(shifted[:, u, :], meta[:, s, :, 0], 7, None, ALU.arith_shift_right).then_inc(s_shift, 1)
                if old:
                    dve.wait_ge(s_ranked, k)
                    at_least(dve, s_base, k - 1)
                    at_least(dve, s_mine, k - 2)
                    nc.vector.tensor_tensor(place[:, v, :, :], ps_p[v][:, 0:CH * NBP].rearrange("p (j b) -> p j b", b=NBP),
                                            g.base[:, :].unsqueeze(1).to_broadcast([P, CH, NBP]), ALU.add).then_inc(s_place, 1)
                if new:
                    dve.wait_ge(s_rel, k + 1)
                    at_least(dve, s_out_of, k - 1)
                    nc.vector.scalar_tensor_tensor(far[:, u, 0, :], rel[:, u, :], -(P - 1.0), rel[:, u, :], ALU.add, ALU.mult).then_inc(s_far, 1)
                if old:
                    dve.wait_ge(s_place, k)
                    nc.vector.tensor_tensor(g.base[:, :], g.base[:, :], ps_p[v][:, CH * NBP:(CH + 1) * NBP], ALU.add).then_inc(s_base, 1)
                if new:
                    dve.wait_ge(s_far, k + 1)
                    at_least(dve, s_to, k - 1)
                    nc.vector.tensor_scalar(far[:, u, 1, :], far[:, u, 0, :], 0.0, SKIP, ALU.is_gt, ALU.mult).then_inc(s_out_of, 1)
                if old:
                    at_least(dve, s_pos, k - 2)
                    nc.vector.tensor_tensor(mine[:, v, :, :], place[:, v, :, :], of[:, v, :, :], ALU.mult).then_inc(s_mine, 1)
                if new:
                    dve.wait_ge(s_out_of, k + 1)
                    dve.wait_ge(s_shift, k + 1)
                    at_least(dve, s_of, k - 1)
                    nc.vector.tensor_tensor(blk[:, u, :], shifted[:, u, :], far[:, u, 1, :], ALU.add).then_inc(s_blk, 1)
                if old:
                    dve.wait_ge(s_mine, k)
                    at_least(dve, s_to, k - 2)
                    nc.vector.tensor_reduce(pos[:, v, :], mine[:, v, :, :], axis=AX.X, op=ALU.add).then_inc(s_pos, 1)
                if new:
                    dve.wait_ge(s_blk, k + 1)
                    at_least(dve, s_ranked, k - 1)
                    at_least(dve, s_mine, k - 1)
                    nc.vector.tensor_tensor(of[:, u, :, :], g.iota[:, 0:NBP].unsqueeze(1).to_broadcast([P, CH, NBP]),
                                            blk[:, u, :].unsqueeze(2).to_broadcast([P, CH, NBP]), ALU.is_equal).then_inc(s_of, 1)
                if old:
                    dve.wait_ge(s_pos, k)
                    nc.vector.tensor_tensor(to[:, (c - 1) % SLOTS, :], pos[:, v, :], far[:, v, 1, :], ALU.add).then_inc(s_to, 1)
                if new:
                    nc.vector.tensor_copy(rec[:, s, :, RW - 1], meta[:, s, :, 0]).then_inc(s_src, 1)

            skewed(dve, step)


def sum_stage(nc, g):
    with ExitStack() as ctx:
        def sb(name, shape, dt=f32):
            return ctx.enter_context(nc.sbuf_tensor(name, shape, dt))

        def sem(name):
            return ctx.enter_context(nc.semaphore(name))

        def upper(words):
            return words.bitcast(bf16)[:, :, 1::2]

        rec = sb("rec3", [P, SLOTS, CH, RW])
        left = sb("left", [P, DEPTH, 2, CH, D])
        rel = sb("rel3", [P, DEPTH, CH])
        apart = sb("apart3", [P, EARLY, P], bf16)
        hot = sb("hot3", [P, DEPTH, CH, P], bf16)
        ps_a = [ctx.enter_context(nc.psum_tensor(f"ps_a{i}", [P, 512], f32)) for i in range(DEPTH)]
        rec_in = [sem(f"rec_in{i}") for i in range(SLOTS)]
        s_rel, s_left, s_rest, s_apart, s_hot_a, s_hot_b, s_sum, s_acc = (
            sem(f"sm_{n}") for n in ("rel", "left", "rest", "apart", "hot_a", "hot_b", "sum", "acc"))
        block = ctx.enter_context(nc.Block())

        @block.sync
        def _(sp):
            def load(i, c):
                s, k = c % SLOTS, i * SLOTS + c
                e0 = sp.value_load(g.e0t[0:1, SRC, bass.ds(k, 1)], min_val=0, max_val=E)
                at_least(sp, s_sum, k - SLOTS + 1)
                sp.dma_start(rec[:, s, :, :], g.rec_d[bass.ds(e0, IT), :].rearrange("(p j) w -> p j w", p=P)).then_inc(rec_in[s], 16)

            ahead(sp, load)

        @block.gpsimd
        def _(pool):
            def step(i, c):
                k = i * SLOTS + c
                if not item(i, c):
                    return
                u = c % DEPTH
                pool.wait_ge(s_left, k + 1)
                at_least(pool, s_sum, k - DEPTH + 1)
                nc.gpsimd.tensor_tensor(left[:, u, 1, :, :], left[:, u, 0, :, :], upper(left[:, u, 0, :, :]), ALU.subtract).then_inc(s_rest, 1)

            skewed(pool, step)

        @block.scalar
        def _(act):
            def step(i, c):
                k = i * SLOTS + c
                if not item(i, c):
                    return
                u = c % DEPTH
                act.wait_ge(s_rel, k + 1)
                at_least(act, s_hot_a, k)
                for j in range(EARLY):
                    apart_j = nc.scalar.activation(apart[:, j, :], g.iotab[:, :], ACT.Abs, scale=-1.0, bias=rel[:, u, j:j + 1])
                apart_j.then_inc(s_apart, 1)
                act.wait_ge(s_apart, k + 1)
                at_least(act, s_sum, k - DEPTH + 1)
                nc.scalar.activation(hot[:, u, 0:EARLY, :], apart[:, :, :], ACT.Relu, scale=-1.0, bias=1.0).then_inc(s_hot_a, 1)

            skewed(act, step)

        @block.tensor
        def _(pe):
            def step(i, c):
                k = i * SLOTS + c
                if not item(i, c):
                    return
                u, s = c % DEPTH, c % SLOTS
                parts = (rec[:, s, :, 0:D], left[:, u, 0, :, :], left[:, u, 1, :, :])
                pe.wait_ge(s_hot_a, k + 1)
                pe.wait_ge(s_hot_b, k + 1)
                at_least(pe, s_acc, k - DEPTH + 1)
                for h in range(PARTS):
                    if h > 0:
                        pe.wait_ge((s_left, s_rest)[h - 1], k + 1)
                    for j in range(CH):
                        mm = nc.tensor.matmul(ps_a[u][:, 0:D], hot[:, u, j, :], upper(parts[h])[:, j, :],
                                              start=h == j == 0, stop=h == PARTS - 1 and j == CH - 1)
                mm.then_inc(s_sum, 1)

            skewed(pe, step)

        @block.vector
        def _(dve):
            def step(i, c):
                k = i * SLOTS + c
                u, v, s = c % DEPTH, (c - 2) % DEPTH, c % SLOTS
                if item(i, c):
                    dve.wait_ge(rec_in[s], after(i, c, 16))
                    at_least(dve, s_sum, k - DEPTH + 1)
                    nc.vector.tensor_scalar(rel[:, u, :], rec[:, s, :, RW - 1], g.b128[:, SRC, bass.ds(k, 1)], None, ALU.subtract).then_inc(s_rel, 1)
                    nc.vector.tensor_tensor(left[:, u, 0, :, :], rec[:, s, :, 0:D], upper(rec[:, s, :, 0:D]), ALU.subtract).then_inc(s_left, 1)
                b = bass.ds(dve.value_load(g.bt[0:1, SRC, bass.ds(k - 2, 1)], min_val=0, max_val=NB), 1) if item(i, c - 2) else None
                if item(i, c):
                    dve.wait_ge(s_rel, k + 1)
                    for j in range(EARLY, CH):
                        hot_j = nc.vector.tensor_scalar(hot[:, u, j, :], g.iotab[:, :], rel[:, u, j:j + 1], None, ALU.is_equal)
                    hot_j.then_inc(s_hot_b, 1)
                if b is not None:
                    dve.wait_ge(s_sum, k - 1)
                    at_least(dve, s_acc, k - 2)
                    nc.vector.tensor_tensor(g.sums[:, b, :], g.sums[:, b, :], ps_a[v][:, 0:D].unsqueeze(1), ALU.add).then_inc(s_acc, 1)

            skewed(dve, step)


def norm_store_stage(nc, g, out):
    with ExitStack() as ctx:
        def sb(name, shape, dt=f32):
            return ctx.enter_context(nc.sbuf_tensor(name, shape, dt))

        def sem(name):
            return ctx.enter_context(nc.semaphore(name))

        st = sb("n2_st", [P, 6, NB])
        square = sb("n2_square", [P, NG, D])
        s_new, s_mean, s_sq, s_var, s_root, s_rstd, s_norm, s_out = (
            sem(f"ns_{n}") for n in ("sum", "mean", "squares", "variance", "root", "rstd", "normed", "stored"))
        block = ctx.enter_context(nc.Block())
        groups = [range(b, min(b + NG, NB)) for b in range(0, NB, NG)]

        def stat(i, bs):
            return st[:, i, bs[0]:bs[-1] + 1]

        @block.sync
        def _(sp):
            for q, bs in enumerate(groups):
                sp.wait_ge(s_norm, q + 1)
                full = [b for b in bs if (b + 1) * P <= N]
                if full:
                    sp.dma_start(out[full[0] * P:(full[-1] + 1) * P, :].rearrange("(b p) d -> p b d", p=P),
                                 g.sums[:, full[0]:full[-1] + 1, :]).then_inc(s_out, 16)
            if LAST < P:
                sp.dma_start(out[(NB - 1) * P:N, :], g.sums[0:LAST, NB - 1, :]).then_inc(s_out, 16)
            stores = sum(1 for bs in groups if (bs[0] + 1) * P <= N) + (LAST < P)
            sp.wait_ge(s_out, 16 * stores)

        @block.scalar
        def _(act):
            for q in range(len(groups) + 1):
                if q > 0:
                    act.wait_ge(s_var, q)
                    nc.scalar.activation(stat(4, groups[q - 1]), stat(3, groups[q - 1]), ACT.Sqrt).then_inc(s_root, 1)
                if q < len(groups):
                    act.wait_ge(s_mean, q + 1)
                    at_least(act, s_sq, q)
                    for n, b in enumerate(groups[q]):
                        sq = nc.scalar.activation(square[:, n, :], g.sums[:, b, :], ACT.Square, bias=st[:, 1, b:b + 1], accum_out=st[:, 2, b:b + 1])
                    sq.then_inc(s_sq, 1)

        @block.vector
        def _(dve):
            for q in range(len(groups) + 1):
                if q < len(groups):
                    new = groups[q]
                    nc.vector.tensor_reduce(stat(0, new), g.sums[:, new[0]:new[-1] + 1, :], axis=AX.X, op=ALU.add).then_inc(s_new, 1)
                    dve.wait_ge(s_new, q + 1)
                    nc.vector.tensor_scalar(stat(1, new), stat(0, new), -1.0 / D, None, ALU.mult).then_inc(s_mean, 1)
                if q > 0:
                    old = groups[q - 1]
                    dve.wait_ge(s_sq, q)
                    nc.vector.tensor_scalar(stat(3, old), stat(2, old), 1.0 / D, EPS, ALU.mult, ALU.add).then_inc(s_var, 1)
                    dve.wait_ge(s_root, q)
                    nc.vector.reciprocal(stat(5, old), stat(4, old)).then_inc(s_rstd, 1)
                    dve.wait_ge(s_rstd, q)
                    dve.wait_ge(s_mean, q)
                    for b in old:
                        row = nc.vector.tensor_scalar(g.sums[:, b, :], g.sums[:, b, :], st[:, 1, b:b + 1], st[:, 5, b:b + 1], ALU.add, ALU.mult)
                    row.then_inc(s_norm, 1)


def gnn_two_layers(nc, xn, xt, w, wt, a2, wm, wr, bm, br, src_h, dst_h, meta_h, feat_h, out):
    with ExitStack() as ctx:
        def sb(name, shape, dt=f32):
            return ctx.enter_context(nc.sbuf_tensor(name, shape, dt))

        g = Shared()
        g.table_d = nc.dram_tensor("node_table", (NP, TW), f32).ap()
        g.rec_d = nc.dram_tensor("records", (E + IT, RW), f32).ap()
        g.x = sb("x", [P, NBP, D])
        first = sb("first", [P, NBP, PARTS * D // 2])
        g.acc = first[:, :, 0:SW]
        g.parts = first[:, :, :].bitcast(bf16).rearrange("p b (h d) -> p b h d", h=PARTS)
        second = sb("second", [P, NBP, TW])
        g.table = second[:, :, :]
        g.sums = second[:, :, 0:D]
        g.erm = sb("erm", [P, NBP, 2])
        g.erm_parts = sb("erm_parts", [P, NBP, PARTS, 2], bf16)
        g.ermin = sb("ermin", [P, NBP, 1])
        g.elmin = sb("elmin", [P, 1])
        g.ident = sb("ident", [P, P])
        g.identb = sb("identb", [P, P], bf16)
        g.ones = sb("ones", [P, P])
        g.iota = sb("iota", [P, 512])
        g.iotab = sb("iotab", [P, P], bf16)
        g.wmr = sb("wmr", [P, 2 * D])
        g.wm2 = sb("wm2", [FE, D])
        g.brow = sb("brow", [1, 3, D])
        g.b128 = sb("b128", [P, 2, KC])
        g.e0t = sb("e0t", [1, 2, KC], i32)
        g.bt = sb("bt", [1, 2, KC], i32)
        g.filled = sb("filled", [1, KC], i32)
        g.moved = sb("moved", [1, KC], i32)
        g.onesb = sb("onesb", [P, P], bf16)
        g.tri = sb("tri", [P, P], bf16)
        g.part = sb("part", [P, 1])
        g.nid = sb("nid", [P, KC])
        g.base = sb("base", [P, NBP])
        setup_stage(nc, g, xn, xt, w, wt, a2, wm, wr, bm, br, src_h, dst_h)
        first_layer_stage(nc, g, meta_h)
        norm_project_stage(nc, g)
        record_stage(nc, g, meta_h, dst_h, feat_h)
        sum_stage(nc, g)
        norm_store_stage(nc, g, out)


def kernel(x, src, dst, edge_attr_32, edge_attr_32_n2, L0_gnn_W, L0_gnn_a_left, L0_gnn_a_right,
           L1_gnn_Wm, L1_gnn_bm, L1_gnn_Wr, L1_gnn_br):
    import numpy as np
    import concourse.bacc as bacc
    from concourse.bass_utils import run_bass_kernel_spmd

    def rows(a, n, fill):
        a = np.asarray(a)
        return np.concatenate([a, np.full((n - len(a),) + a.shape[1:], fill, a.dtype)])

    xp = rows(x, NP, 0)
    sp, dp = rows(src, EP, PAD_NODE), rows(dst, EP, PAD_NODE)
    ins = {
        "xn": xp, "xt": np.ascontiguousarray(xp.T),
        "w": np.asarray(L0_gnn_W), "wt": np.ascontiguousarray(np.asarray(L0_gnn_W).T),
        "a2": np.ascontiguousarray(np.concatenate([np.asarray(L0_gnn_a_left), np.asarray(L0_gnn_a_right)]).T),
        "wm": np.asarray(L1_gnn_Wm), "wr": np.asarray(L1_gnn_Wr),
        "bm": np.asarray(L1_gnn_bm)[None, :], "br": np.asarray(L1_gnn_br)[None, :],
        "src_h": sp, "dst_h": dp, "meta_h": np.stack([sp, dp], axis=1),
        "feat_h": np.ascontiguousarray(rows(np.concatenate([np.asarray(edge_attr_32), np.asarray(edge_attr_32_n2)], axis=1), EP, 0).T),
    }
    nc = bacc.Bacc("TRN2", target_bir_lowering=False, num_devices=1)
    args = [nc.dram_tensor(n, a.shape, mybir.dt.from_np(a.dtype), kind="ExternalInput").ap() for n, a in ins.items()]
    args.append(nc.dram_tensor("out", (N, D), f32, kind="ExternalOutput").ap())
    gnn_two_layers(nc, *args)
    r = run_bass_kernel_spmd(nc, [ins], core_ids=[0])
    return r.results[0]["out"]
```
